# Optimizing a Trainium2 kernel written in Bass

```python
import numpy as np
import jax
import jax.numpy as jnp

def _softmax(x, axis=-1):
    return jax.nn.softmax(x, axis=axis)

def _gelu(x):
    return jax.nn.gelu(x, approximate=True)

def _silu(x):
    return jax.nn.silu(x)

def _sigmoid(x):
    return jax.nn.sigmoid(x)

def _layernorm(x, axis=-1, eps=1e-05):
    m = jnp.mean(x, axis=axis, keepdims=True)
    v = jnp.var(x, axis=axis, keepdims=True)
    return (x - m) / jnp.sqrt(v + eps)

def _scatter_add(tgt, idx, src, axis=0):
    return tgt.at[idx].add(src)

def _segment_sum(src, seg, n):
    return jax.ops.segment_sum(src, seg, n)
kernel_name = 'mk_perceiver_d1_seqx_r2_850773'

def setup_inputs(seed: int=0):
    np.random.seed(seed)
    _w = jnp.asarray

    def _rec_inputs():
        import jax
        import jax.numpy as jnp
        _rk = jax.random.key(seed)
        x = -0.0002928 + 1 * jax.random.normal(jax.random.fold_in(_rk, 1), (64, 32, 512), jnp.float32)
        _lenS = 32 - jax.random.randint(jax.random.fold_in(_rk, 7), (64,), 0, max(1, 32 // 4) + 1, jnp.int32)
        _lenS2 = 257 - jax.random.randint(jax.random.fold_in(_rk, 8), (64,), 0, max(1, 257 // 4) + 1, jnp.int32)
        _ctx_1024P = jax.random.normal(jax.random.fold_in(_rk, 11), (64, 16, 512), jnp.float32)
        _ctx_1024c = jax.random.dirichlet(jax.random.fold_in(_rk, 511), 0.3 * jnp.ones((16,), jnp.float32), (64, 257))
        _ctx_1024t = jnp.einsum('bsk,bkd->bsd', _ctx_1024c, _ctx_1024P)
        _ctx_1024t = _ctx_1024t * jax.lax.rsqrt(jnp.mean(jnp.square(_ctx_1024t)) + 1e-12) * 0.953939
        ctx_1024 = 4.13588e-05 + 0.999923 * (_ctx_1024t + 0.3 * jax.random.normal(jax.random.fold_in(_rk, 611), (64, 257, 512), jnp.float32))
        return (x, ctx_1024)
    x, ctx_1024 = _rec_inputs()

    def _L0_xattn_setup():
        import jax, jax.numpy as jnp
        import numpy as np
        DIM = 512
        NUM_HEADS = 16
        DIM_HEAD = 64
        INNER = NUM_HEADS * DIM_HEAD
        SCALE = DIM_HEAD ** (-0.5)

        def _layernorm(x, gamma, beta, eps=1e-05):
            mu = jnp.mean(x, axis=-1, keepdims=True)
            var = jnp.mean(jnp.square(x - mu), axis=-1, keepdims=True)
            return (x - mu) * jax.lax.rsqrt(var + eps) * gamma + beta
        key = jax.random.key(seed)
        ks = jax.random.split(key, 8)
        B, SQ, SK = (2, 1024, 2048)
        x = jax.random.normal(ks[0], (B, SQ, DIM), dtype=jnp.float32)
        context = jax.random.normal(ks[1], (B, SK, DIM), dtype=jnp.float32)
        ln_gamma = jnp.ones((DIM,), jnp.float32)
        ln_beta = jnp.zeros((DIM,), jnp.float32)
        w_q = jax.random.normal(ks[2], (DIM, INNER), dtype=jnp.float32) / np.sqrt(DIM)
        w_kv = jax.random.normal(ks[3], (DIM, 2 * INNER), dtype=jnp.float32) / np.sqrt(DIM)
        w_out = jax.random.normal(ks[4], (INNER, DIM), dtype=jnp.float32) / np.sqrt(INNER)
        b_out = jnp.zeros((DIM,), jnp.float32)
        gate = jnp.array([0.5], jnp.float32)
        return {'x': x, 'context': context, 'ln_gamma': ln_gamma, 'ln_beta': ln_beta, 'w_q': w_q, 'w_kv': w_kv, 'w_out': w_out, 'b_out': b_out, 'gate': gate}
    _L0_xattn_all = _L0_xattn_setup()
    _L0_xattn_in = {k: v for k, v in _L0_xattn_all.items() if k in ('ln_gamma', 'ln_beta', 'w_q', 'w_kv', 'w_out', 'b_out', 'gate')}
    del _L0_xattn_all

    def _L0_attn_setup():
        import jax, jax.numpy as jnp
        import numpy as np
        DIMS = 512
        HEADS = 16
        HEAD_DIM = DIMS // HEADS
        key = jax.random.key(seed)
        k_x, k_q, k_k, k_v = jax.random.split(key, 4)
        scale = 1.0 / np.sqrt(DIMS)
        return {'input_seq_embs': jax.random.normal(k_x, (4, 2048, DIMS), dtype=jnp.float32), 'W_Q': jax.random.normal(k_q, (DIMS, DIMS), dtype=jnp.float32) * scale, 'W_K': jax.random.normal(k_k, (DIMS, DIMS), dtype=jnp.float32) * scale, 'W_V': jax.random.normal(k_v, (DIMS, DIMS), dtype=jnp.float32) * scale}
    _L0_attn_all = _L0_attn_setup()
    _L0_attn_in = {k: v for k, v in _L0_attn_all.items() if k in ('W_Q', 'W_K', 'W_V')}
    del _L0_attn_all

    def _L0_ffn_setup():
        import jax, jax.numpy as jnp
        import numpy as np
        DIM = 512
        HIDDEN = 1536
        SCALE = 1.0 / 127.0

        def _dequant(w_int, dtype):
            return w_int.astype(dtype) * jnp.asarray(SCALE, dtype)
        key = jax.random.key(seed)
        k_x, k_g, k_u, k_d = jax.random.split(key, 4)
        x = jax.random.normal(k_x, (4, 1024, DIM), dtype=jnp.float32)
        w_gate = jax.random.randint(k_g, (HIDDEN, DIM), -127, 128, dtype=jnp.int32)
        w_up = jax.random.randint(k_u, (HIDDEN, DIM), -127, 128, dtype=jnp.int32)
        w_down = jax.random.randint(k_d, (DIM, HIDDEN), -127, 128, dtype=jnp.int32)
        return {'x': x, 'w_gate': w_gate, 'w_up': w_up, 'w_down': w_down}
    _L0_ffn_all = _L0_ffn_setup()
    _L0_ffn_in = {k: v for k, v in _L0_ffn_all.items() if k in ('w_gate', 'w_up', 'w_down')}
    del _L0_ffn_all
    return {'x': x, 'ctx_1024': ctx_1024, 'L0_xattn_ln_gamma': _L0_xattn_in['ln_gamma'], 'L0_xattn_ln_beta': _L0_xattn_in['ln_beta'], 'L0_xattn_w_q': _L0_xattn_in['w_q'], 'L0_xattn_w_kv': _L0_xattn_in['w_kv'], 'L0_xattn_w_out': _L0_xattn_in['w_out'], 'L0_xattn_b_out': _L0_xattn_in['b_out'], 'L0_xattn_gate': _L0_xattn_in['gate'], 'L0_attn_W_Q': _L0_attn_in['W_Q'], 'L0_attn_W_K': _L0_attn_in['W_K'], 'L0_attn_W_V': _L0_attn_in['W_V'], 'L0_ffn_w_gate': _L0_ffn_in['w_gate'], 'L0_ffn_w_up': _L0_ffn_in['w_up'], 'L0_ffn_w_down': _L0_ffn_in['w_down']}

def reference(x, ctx_1024, L0_xattn_ln_gamma, L0_xattn_ln_beta, L0_xattn_w_q, L0_xattn_w_kv, L0_xattn_w_out, L0_xattn_b_out, L0_xattn_gate, L0_attn_W_Q, L0_attn_W_K, L0_attn_W_V, L0_ffn_w_gate, L0_ffn_w_up, L0_ffn_w_down):
    import jax
    import jax.numpy as jnp

    def _L0_xattn_ref(x, context, ln_gamma, ln_beta, w_q, w_kv, w_out, b_out, gate):
        import jax, jax.numpy as jnp
        import numpy as np
        DIM = 512
        NUM_HEADS = 16
        DIM_HEAD = 64
        INNER = NUM_HEADS * DIM_HEAD
        SCALE = DIM_HEAD ** (-0.5)

        def _layernorm(x, gamma, beta, eps=1e-05):
            mu = jnp.mean(x, axis=-1, keepdims=True)
            var = jnp.mean(jnp.square(x - mu), axis=-1, keepdims=True)
            return (x - mu) * jax.lax.rsqrt(var + eps) * gamma + beta
        B, SQ, _ = x.shape
        SK = context.shape[1]
        xn = _layernorm(x, ln_gamma, ln_beta)
        q = (xn @ w_q).reshape(B, SQ, NUM_HEADS, DIM_HEAD)
        kv = context @ w_kv
        k, v = jnp.split(kv, 2, axis=-1)
        k = k.reshape(B, SK, NUM_HEADS, DIM_HEAD)
        v = v.reshape(B, SK, NUM_HEADS, DIM_HEAD)
        scores = jnp.einsum('bqhd,bkhd->bhqk', q * SCALE, k)
        attn = jax.nn.softmax(scores, axis=-1)
        out = jnp.einsum('bhqk,bkhd->bqhd', attn, v).reshape(B, SQ, INNER)
        out = out @ w_out + b_out
        return out * jnp.tanh(gate[0])

    def _L0_attn_ref(input_seq_embs, W_Q, W_K, W_V):
        import jax, jax.numpy as jnp
        import numpy as np
        DIMS = 512
        HEADS = 16
        HEAD_DIM = DIMS // HEADS
        B, L, d = input_seq_embs.shape
        H, hd = (HEADS, HEAD_DIM)
        Q = (input_seq_embs @ W_Q.T).reshape(B, L, H, hd)
        K = (input_seq_embs @ W_K.T).reshape(B, L, H, hd)
        V = (input_seq_embs @ W_V.T).reshape(B, L, H, hd)
        sK = jax.nn.softmax(jnp.swapaxes(K, -1, -2), axis=-1)
        tran_V = jnp.einsum('bldh,blhe->blde', sK, V)
        out = jnp.einsum('blhd,blde->blhe', jax.nn.softmax(Q, axis=-1), tran_V)
        return out.reshape(B, L, d)

    def _L0_ffn_ref(x, w_gate, w_up, w_down):
        import jax, jax.numpy as jnp
        import numpy as np
        DIM = 512
        HIDDEN = 1536
        SCALE = 1.0 / 127.0

        def _dequant(w_int, dtype):
            return w_int.astype(dtype) * jnp.asarray(SCALE, dtype)
        wg = _dequant(w_gate, x.dtype)
        wu = _dequant(w_up, x.dtype)
        wd = _dequant(w_down, x.dtype)
        gate = jnp.einsum('bsd,hd->bsh', x, wg)
        up = jnp.einsum('bsd,hd->bsh', x, wu)
        h = jax.nn.silu(gate) * up
        return jnp.einsum('bsh,dh->bsd', h, wd)
    x = x + _L0_xattn_ref(_layernorm(x, axis=-1), ctx_1024, L0_xattn_ln_gamma, L0_xattn_ln_beta, L0_xattn_w_q, L0_xattn_w_kv, L0_xattn_w_out, L0_xattn_b_out, L0_xattn_gate)
    x = x + _L0_attn_ref(_layernorm(x, axis=-1), L0_attn_W_Q, L0_attn_W_K, L0_attn_W_V)
    x = x + _L0_ffn_ref(_layernorm(x, axis=-1), L0_ffn_w_gate, L0_ffn_w_up, L0_ffn_w_down)
    return x

_drawn_inputs = setup_inputs


def setup_inputs(seed=0):
    import zlib

    import numpy as np

    out = dict(_drawn_inputs(seed))
    spreads = {'L0_xattn_ln_gamma': (1.0, 0.55),
     'L0_xattn_ln_beta': (0.0, 0.578),
     'L0_xattn_b_out': (0.0, 0.1)}
    factors = {}
    for name, (base, spread) in spreads.items():
        noise = np.random.default_rng([zlib.crc32(name.encode()), seed]).standard_normal(out[name].shape)
        drawn = base * np.exp(spread * noise) if base else spread * noise
        out[name] = jnp.asarray(drawn.astype(out[name].dtype))
    for name, factor in factors.items():
        out[name] = (out[name] * factor).astype(out[name].dtype)
    return out
```

```python
from contextlib import ExitStack

import concourse.bass as bass
from concourse import mybir

ALU = mybir.AluOpType
ACT = mybir.ActivationFunctionType
F32 = mybir.dt.float32
F32R = mybir.dt.float32r
AX_X = mybir.AxisListType.X
P = 128
EPS = 1e-5


class Count:

    def __init__(self, sem, per, credit=0):
        self.sem, self.per, self.credit = sem, per, credit

    def at(self, turn, n):
        assert self.credit + n > 0
        return turn * self.per + (self.credit + n)


class Chain:

    def __init__(self, eng, sem, turn, per):
        self.eng, self.sem, self.turn, self.per, self.n = eng, sem, turn, per, 0

    def step(self, ins):
        self.n += 1
        ins.then_inc(self.sem, 1)
        self.eng.wait_ge(self.sem, self.turn * self.per + self.n)


class Scope:

    def __init__(self, nc, ctx, name):
        self.nc, self.ctx, self.name = nc, ctx, name

    def sb(self, name, shape, dt=F32):
        return self.ctx.enter_context(self.nc.sbuf_tensor(f"{self.name}_{name}", shape, dt))

    def pair(self, name, shape):
        return self.sb(name + "_hi", shape, F32R), self.sb(name + "_lo", shape, F32R)

    def psum(self):
        return self.ctx.enter_context(self.nc.psum_tensor(f"{self.name}_ps", [P, 8, 512], F32))

    def sem(self, name):
        return self.ctx.enter_context(self.nc.semaphore(f"{self.name}_{name}"))

    def count(self, name, per, credit=0):
        return Count(self.sem(name), per, credit)


def f32(ap):
    return ap.bitcast(F32)


def three(pe, out, lhs, rhs, start, stop):
    pe.matmul(out, lhs[0], rhs[0], start=start, stop=False)
    pe.matmul(out, lhs[0], rhs[1], start=False, stop=False)
    return pe.matmul(out, lhs[1], rhs[0], start=False, stop=stop)


def load_split(nc, name, pieces, width, dt=F32, scale=1.0):
    with ExitStack() as ctx:
        s = Scope(nc, ctx, name)
        raw = [s.sb(f"raw{i}", [P, width], dt) for i in range(2)]
        loaded = [s.sem(f"loaded{i}") for i in range(2)]
        hi_done, lo_done = s.sem("hi_done"), s.sem("lo_done")
        block = ctx.enter_context(nc.Block())

        @block.sync
        def _(sp):
            for n, (src, hi, lo) in enumerate(pieces):
                if n >= 2:
                    sp.wait_ge(lo_done, n - 1)
                sp.dma_start(raw[n % 2][:, :], src).then_inc(loaded[n % 2], 16)

        @block.scalar
        def _(act):
            for n, (src, hi, lo) in enumerate(pieces):
                act.wait_ge(loaded[n % 2], 16 * (n // 2 + 1))
                act.activation(hi, raw[n % 2][:, :], ACT.Copy, scale=scale).then_inc(hi_done, 1)

        @block.vector
        def _(dve):
            for n, (src, hi, lo) in enumerate(pieces):
                dve.wait_ge(loaded[n % 2], 16 * (n // 2 + 1))
                dve.wait_ge(hi_done, n + 1)
                dve.scalar_tensor_tensor(lo, raw[n % 2][:, :], scale, f32(hi), ALU.mult,
                                         ALU.subtract).then_inc(lo_done, 1)


def weight_pieces(src, hi, lo, width):
    n = src.shape[1]
    assert n % width == 0
    return [(src[:, i:i + width], hi[:, i:i + width], lo[:, i:i + width]) for i in range(0, n, width)]


def norm_moments(dve, chain, src, stats, moments, shifted, tiles, asked):
    for i in range(tiles):
        ins = dve.bn_stats(stats[:, i, :], src[:, i, :])
    chain.step(ins)
    dve.memset(shifted[:, 0:tiles], EPS)
    for i in range(tiles):
        ins = dve.bn_aggr(moments[:, i, :], stats[:, i, :])
    chain.step(ins)
    dve.tensor_tensor(shifted[:, 0:tiles], shifted[:, 0:tiles], moments[:, 0:tiles, 1], ALU.add)\
        .then_inc(asked.sem, 1)


def norm_scale(dve, dst, src, moments, rstd, tiles):
    for i in range(tiles):
        ins = dve.tensor_scalar(dst[:, i, :], src[:, i, :], moments[:, i, 0:1], rstd[:, i:i + 1],
                                ALU.subtract, ALU.mult)
    return ins


def project_queries(nc, x, gamma, beta, wq, q_hi, q_lo, identity, scale):
    tokens, dim = x.shape
    inner = wq.shape[1]
    DC, PAIRS, TT = dim // P, inner // P, 4
    N = TT * P
    TURNS = tokens // N
    with ExitStack() as ctx:
        s = Scope(nc, ctx, "q")
        w = s.pair("wq", [P, DC * inner])
        wsrc = wq.rearrange("(c p) n -> c p n", p=P)
        pieces = [(wsrc[c], w[0][:, c * inner:(c + 1) * inner], w[1][:, c * inner:(c + 1) * inner]) for c in range(DC)]
        load_split(nc, "qw", pieces, inner)
        wt = [t[:, :].rearrange("p (c n) -> p c n", c=DC) for t in w]

        xin, xn, xn2 = s.sb("xin", [P, TT, dim]), s.sb("xn", [P, TT, dim]), s.sb("xn2", [P, TT, dim])
        stats, moments = s.sb("stats", [P, TT, 6]), s.sb("moments", [P, TT, 2])
        shifted, rstd, power = s.sb("shifted", [P, TT]), s.sb("rstd", [P, TT]), s.sb("power", [P, TT])
        ident = s.sb("ident", [P, P])
        g, b = s.sb("gamma", [P, DC]), s.sb("beta", [P, DC])
        affine = s.sb("affine", [P, DC, N])
        xT = s.pair("xT", [P, DC, N])
        q = s.pair("q", [P, PAIRS, N])
        ps = s.psum()
        once, x_loaded, q_stored = s.sem("once"), s.count("x_loaded", 16), s.count("q_stored", 32, 32)
        normed = s.count("normed", 1, 1)
        DVE_STEPS = 5
        dve_chain = s.sem("dve_chain")
        var_ready, rstd_done, power_set = s.count("var_ready", 2), s.count("rstd_done", 2), s.sem("power_set")
        turned, affine_done = s.count("turned", DC), s.count("affine_done", DC, 0)
        xhi_done, xlo_done = s.count("xhi_done", DC), s.count("xlo_done", DC)
        q_ready, qhi_done, qlo_done = s.count("q_ready", PAIRS), s.count("qhi_done", PAIRS), s.count("qlo_done", PAIRS)
        block = ctx.enter_context(nc.Block())

        @block.sync
        def _(sp):
            sp.dma_start(ident[:, :], identity).then_inc(once, 16)
            sp.dma_start(g[:, :], gamma).then_inc(once, 16)
            sp.dma_start(b[:, :], beta).then_inc(once, 16)
            with sp.Fori(0, TURNS) as t:
                sp.wait_ge(normed.sem, normed.at(t, 0))
                sp.dma_start(xin[:, :, :], x[bass.ds(t * N, N), :].rearrange("(i p) d -> p i d", p=P))\
                    .then_inc(x_loaded.sem, 16)

        @block.gpsimd
        def _(pool):
            pool.memset(power[:, :], -0.5).then_inc(power_set, 1)
            pool.wait_ge(power_set, 1)
            with pool.Fori(0, TURNS) as t:
                for k in range(2):
                    pool.wait_ge(var_ready.sem, var_ready.at(t, k + 1))
                    pool.tensor_tensor(rstd[:, :], shifted[:, :], power[:, :], ALU.pow).then_inc(rstd_done.sem, 1)

        @block.vector
        def _(dve):
            dve.sem_inc(normed.sem, 1)
            dve.wait_ge(once, 48)
            with dve.Fori(0, TURNS) as t:
                chain = Chain(dve, dve_chain, t, DVE_STEPS)
                dve.wait_ge(x_loaded.sem, x_loaded.at(t, 16))
                norm_moments(dve, chain, xin, stats, moments, shifted, TT, var_ready)
                dve.wait_ge(rstd_done.sem, rstd_done.at(t, 1))
                chain.step(norm_scale(dve, xn, xin, moments, rstd, TT))
                norm_moments(dve, chain, xn, stats, moments, shifted, TT, var_ready)
                dve.wait_ge(rstd_done.sem, rstd_done.at(t, 2))
                norm_scale(dve, xn2, xn, moments, rstd, TT).then_inc(normed.sem, 1)
                for c in range(DC):
                    dve.wait_ge(turned.sem, turned.at(t, c + 1))
                    dve.tensor_scalar(affine[:, c, :], ps[:, c, :], g[:, c:c + 1], b[:, c:c + 1],
                                      ALU.mult, ALU.add).then_inc(affine_done.sem, 1)
                for c in range(DC):
                    dve.wait_ge(xhi_done.sem, xhi_done.at(t, c + 1))
                    dve.tensor_tensor(xT[1][:, c, :], affine[:, c, :], f32(xT[0][:, c, :]), ALU.subtract)\
                        .then_inc(xlo_done.sem, 1)
                for j in range(PAIRS):
                    dve.wait_ge(qhi_done.sem, qhi_done.at(t, j + 1))
                    dve.scalar_tensor_tensor(q[1][:, j, :], ps[:, 4 + j % 4, :], scale, f32(q[0][:, j, :]),
                                             ALU.mult, ALU.subtract).then_inc(qlo_done.sem, 1)

        @block.scalar
        def _(act):
            act.sem_inc(q_stored.sem, 32)
            with act.Fori(0, TURNS) as t:
                for c in range(DC):
                    act.wait_ge(affine_done.sem, affine_done.at(t, c + 1))
                    act.activation(xT[0][:, c, :], affine[:, c, :], ACT.Copy).then_inc(xhi_done.sem, 1)
                for j in range(PAIRS):
                    act.wait_ge(q_ready.sem, q_ready.at(t, j + 1))
                    if j == 0:
                        act.wait_ge(q_stored.sem, q_stored.at(t, 0))
                    act.activation(q[0][:, j, :], ps[:, 4 + j % 4, :], ACT.Copy, scale=scale)\
                        .then_inc(qhi_done.sem, 1)
                act.wait_ge(qhi_done.sem, qhi_done.at(t, PAIRS))
                act.wait_ge(qlo_done.sem, qlo_done.at(t, PAIRS))
                for dst, src in ((q_hi, q[0]), (q_lo, q[1])):
                    act.dma_start(dst[:, :, bass.ds(t * N, N)].rearrange("j p n -> p j n"), f32(src[:, :, :]))\
                        .then_inc(q_stored.sem, 16)
            act.wait_ge(q_stored.sem, 32 * TURNS + 32)

        @block.tensor
        def _(pe):
            pe.wait_ge(once, 48)
            with pe.Fori(0, TURNS) as t:
                pe.wait_ge(normed.sem, normed.at(t, 1))
                for c in range(DC):
                    for i in range(TT):
                        mm = pe.transpose(ps[:, c, i * P:(i + 1) * P], xn2[:, i, c * P:(c + 1) * P], ident[:, :])
                    mm.then_inc(turned.sem, 1)
                pe.wait_ge(xlo_done.sem, xlo_done.at(t, DC))
                for j in range(PAIRS):
                    if j >= 4:
                        pe.wait_ge(qlo_done.sem, qlo_done.at(t, j - 3))
                    for c in range(DC):
                        mm = three(pe, ps[:, 4 + j % 4, :], [a[:, c, j * P:(j + 1) * P] for a in wt],
                                   [a[:, c, :] for a in xT], c == 0, c == DC - 1)
                    mm.then_inc(q_ready.sem, 1)


def cross_attention(nc, ctx_nat, ctx_T, last_T, wkT, wv, q_hi, q_lo, v_hi, v_lo, o_hi, o_lo, identity, heads):
    B, SK, dim = ctx_nat.shape
    inner = wv.shape[1]
    DC, PAIRS = dim // P, inner // P
    tokens = q_hi.shape[2]
    SQ = tokens // B
    GB = P // SQ
    TURNS = B // GB
    KT = SK // P
    SKE = SK + 1
    HT = P // SQ
    TILES = heads // HT
    HE = inner // heads
    assert SK == KT * P + 1 and TILES == 4 and DC == 4 and KT == 2
    with ExitStack() as ctx:
        s = Scope(nc, ctx, "x")
        wk = s.pair("wk", [P, PAIRS * dim])
        w_v = s.pair("wv", [P, DC * inner])
        wk_src, wv_src = wkT.rearrange("(j p) d -> j p d", p=P), wv.rearrange("(c p) n -> c p n", p=P)
        pieces = [(wk_src[j], wk[0][:, j * dim:(j + 1) * dim], wk[1][:, j * dim:(j + 1) * dim]) for j in range(PAIRS)]
        for c in range(DC):
            for h in range(inner // dim):
                a = c * inner + h * dim
                pieces.append((wv_src[c, :, h * dim:(h + 1) * dim], w_v[0][:, a:a + dim], w_v[1][:, a:a + dim]))
        load_split(nc, "xw", pieces, dim)
        wk = [a[:, :].rearrange("p (j d) -> p j d", j=PAIRS) for a in wk]
        w_v = [a[:, :].rearrange("p (c n) -> p c n", c=DC) for a in w_v]

        last_values(nc, last_T, w_v, v_hi, v_lo)

        fold = s.pair("fold", [P, DC, GB, heads * SQ])
        qz = [s.pair(f"qz{i}", [P, 2, P]) for i in range(2)]
        raw_n, raw_T = s.sb("raw_n", [P, KT, dim]), s.sb("raw_T", [P, DC, SK])
        cn = [s.pair(f"cn{i}", [P, KT, dim]) for i in range(2)]
        cT = [s.pair(f"cT{i}", [P, DC, SKE]) for i in range(2)]
        prob = s.sb("prob", [P, TILES, SKE])
        pT = s.pair("pT", [P, KT, heads * SQ])
        last_p = s.sb("last_p", [P, heads, GB, SQ], F32R)
        last_v = s.sb("last_v", [P, inner], F32R)
        last_z = s.sb("last_z", [P, GB, TILES, GB])
        o = s.pair("o", [P, PAIRS, P])
        ident = s.sb("ident", [P, P])
        negmax, total, share = s.sb("negmax", [P, TILES]), s.sb("total", [P, TILES]), s.sb("share", [P, TILES])
        ps = s.psum()
        S_BANK, T_BANK, L_BANK, M_BANK = (0, 1, 2, 5), (3, 4), 5, (6, 7)
        FOLD_BANK, O_BANK = (3, 4, 6, 7), (0, 1, 2, 5)

        once, cleared, act_cleared = s.sem("once"), s.sem("cleared"), s.sem("act_cleared")
        qz_loaded = [s.count(f"qz_loaded{i}", 64 * PAIRS // 2) for i in range(2)]
        v_loaded = s.count("v_loaded", 48)
        n_loaded, T_loaded = s.count("n_loaded", 16 * GB), s.count("T_loaded", 16 * GB)
        nhi_done, Thi_done = s.count("nhi_done", GB), s.count("Thi_done", GB)
        nlo_done, Tlo_done = s.count("nlo_done", GB, 1), s.count("Tlo_done", GB, 1)
        fold_ready = s.count("fold_ready", 2 * PAIRS, 4)
        fold_hi, fold_lo = s.count("fold_hi", 2 * PAIRS), s.count("fold_lo", 2 * PAIRS)
        scores_ready = s.count("scores_ready", GB * TILES, 2 * TILES)
        max_done, exp_done = s.count("max_done", GB * TILES), s.count("exp_done", GB * TILES)
        share_done, probs_ready = s.count("share_done", GB), s.count("probs_ready", GB)
        turned, last_turned = s.count("turned", GB * KT), s.count("last_turned", GB)
        pT_hi, pT_lo = s.count("pT_hi", GB * KT), s.count("pT_lo", GB * KT)
        last_hi, last_copy, last_lo = s.count("last_hi", GB), s.count("last_copy", GB), s.count("last_lo", GB)
        mixed = s.count("mixed", GB * DC, 2 * DC)
        mixed_hi, mixed_lo = s.count("mixed_hi", GB * DC), s.count("mixed_lo", GB * DC)
        o_ready = s.count("o_ready", PAIRS, 1)
        o_hi_done, o_lo_done = s.count("o_hi_done", 2 * PAIRS), s.count("o_lo_done", 2 * PAIRS, 1)
        o_stored, o_free = s.count("o_stored", 32), s.count("o_free", 1, 1)
        block = ctx.enter_context(nc.Block())

        def pair_of_heads(a, j, u):
            return a[:, 2 * u:2 * u + 2, :, 2 * j * SQ:2 * (j + 1) * SQ].rearrange("p c b n -> p (c b) n")

        @block.sync
        def _(sp):
            sp.dma_start(ident[:, :], identity).then_inc(once, 16)
            sp.wait_ge(cleared, 1)
            with sp.Fori(0, TURNS) as t:
                def load_context(b):
                    sp.wait_ge(Tlo_done.sem, Tlo_done.at(t, b))
                    sp.dma_start(raw_T[:, :, :], ctx_T[t * GB + b].rearrange("(c p) k -> p c k", p=P))\
                        .then_inc(T_loaded.sem, 16)
                    sp.wait_ge(nlo_done.sem, nlo_done.at(t, b))
                    sp.dma_start(raw_n[:, :, :], ctx_nat[t * GB + b, 0:KT * P, :].rearrange("(k p) d -> p k d", p=P))\
                        .then_inc(n_loaded.sem, 16)

                for j in range(PAIRS):
                    sp.wait_ge(fold_ready.sem, fold_ready.at(t, 2 * (j - 1)))
                    for dst, src in zip(qz[j % 2], (q_hi, q_lo)):
                        for h in range(2):
                            sp.dma_start(f32(dst[h * HE:(h + 1) * HE, h, :]),
                                         src[j, h * HE:(h + 1) * HE, bass.ds(t * P, P)])\
                                .then_inc(qz_loaded[j % 2].sem, 16)
                    if j == 1:
                        load_context(0)
                load_context(1)
                sp.wait_ge(o_ready.sem, o_ready.at(t, 0))
                for row, src in ((0, v_hi), (32, v_lo), (64, v_hi)):
                    sp.dma_start(f32(last_v[row:row + GB, :]), src[bass.ds(t * GB, GB), :]).then_inc(v_loaded.sem, 16)
                for b in range(2, GB):
                    load_context(b)

        @block.gpsimd
        def _(pool):
            for ap in [last_z[:, :, :, :]]:
                pool.memset(ap, 0.0)
            for ap in [last_p[:, :, :, :], last_v[:, :]] + [a[:, :, :] for q in qz for a in q] +\
                      [a[:, :, SK:SKE] for c in cT for a in c]:
                last = pool.memset(f32(ap), 0.0)
            last.then_inc(cleared, 1)
            pool.sem_inc(nlo_done.sem, 1)
            pool.sem_inc(Tlo_done.sem, 1)
            pool.sem_inc(o_free.sem, 1)
            with pool.Fori(0, TURNS) as t:
                for b in range(GB):
                    pool.wait_ge(Thi_done.sem, Thi_done.at(t, b + 1))
                    pool.tensor_tensor(cT[b % 2][1][:, :, 0:SK], raw_T[:, :, :], f32(cT[b % 2][0][:, :, 0:SK]),
                                       ALU.subtract).then_inc(Tlo_done.sem, 1)
                    pool.wait_ge(nhi_done.sem, nhi_done.at(t, b + 1))
                    pool.tensor_tensor(cn[b % 2][1][:, :, :], raw_n[:, :, :], f32(cn[b % 2][0][:, :, :]),
                                       ALU.subtract).then_inc(nlo_done.sem, 1)
                pool.wait_ge(o_hi_done.sem, o_hi_done.at(t, 2 * PAIRS))
                pool.wait_ge(o_lo_done.sem, o_lo_done.at(t, 2 * PAIRS))
                for dst, src in zip((o_hi, o_lo), o):
                    pool.dma_start(dst[:, :, bass.ds(t * P, P)].rearrange("j p n -> p j n"), f32(src[:, :, :]))\
                        .then_inc(o_stored.sem, 16)
                pool.wait_ge(o_stored.sem, o_stored.at(t, 32))
                pool.sem_inc(o_free.sem, 1)

        @block.tensor
        def _(pe):
            pe.sem_inc(fold_ready.sem, 4)
            pe.sem_inc(o_ready.sem, 1)
            pe.sem_inc(scores_ready.sem, 2 * TILES)
            pe.sem_inc(mixed.sem, 2 * DC)
            pe.wait_ge(once, 16)
            pe.wait_ge(cleared, 1)
            with pe.Fori(0, TURNS) as t:
                def scores(b):
                    pe.wait_ge(Tlo_done.sem, Tlo_done.at(t, b + 1))
                    for i in range(TILES):
                        if b > 0:
                            pe.wait_ge(exp_done.sem, exp_done.at(t, (b - 1) * TILES + i + 1))
                            if S_BANK[i] == L_BANK:
                                pe.wait_ge(last_copy.sem, last_copy.at(t, b))
                                pe.wait_ge(last_lo.sem, last_lo.at(t, b))
                        for c in range(DC):
                            mm = three(pe, ps[:, S_BANK[i], 0:SKE],
                                       [a[:, c, b, i * P:(i + 1) * P] for a in fold],
                                       [a[:, c, :] for a in cT[b % 2]], c == 0, c == DC - 1)
                        mm.then_inc(scores_ready.sem, 1)

                def turn_probs(b):
                    pe.wait_ge(probs_ready.sem, probs_ready.at(t, b + 1))
                    for k in range(KT):
                        for i in range(TILES):
                            mm = pe.transpose(ps[:, T_BANK[k], i * P:(i + 1) * P], prob[:, i, k * P:(k + 1) * P],
                                              ident[:, :])
                        mm.then_inc(turned.sem, 1)
                    for i in range(TILES):
                        mm = pe.transpose(ps[0:GB, L_BANK, i * P:(i + 1) * P], last_z[:, b, i, :], ident[:, :])
                    mm.then_inc(last_turned.sem, 1)

                def mix(b):
                    pe.wait_ge(pT_lo.sem, pT_lo.at(t, (b + 1) * KT))
                    pe.wait_ge(nlo_done.sem, nlo_done.at(t, b + 1))
                    for c in range(DC):
                        if b > 0 or c >= 2:
                            pe.wait_ge(mixed_lo.sem, mixed_lo.at(t, b * DC + c - 1))
                        for k in range(KT):
                            mm = three(pe, ps[:, M_BANK[c % 2], :],
                                       [a[:, k, c * P:(c + 1) * P] for a in cn[b % 2]],
                                       [a[:, k, :] for a in pT], k == 0, k == KT - 1)
                        mm.then_inc(mixed.sem, 1)

                for j in range(PAIRS):
                    pe.wait_ge(qz_loaded[j % 2].sem, qz_loaded[j % 2].at(t, 64 * (j // 2 + 1)))
                    for u in range(2):
                        n = 2 * j + u
                        if n >= 4:
                            pe.wait_ge(fold_lo.sem, fold_lo.at(t, n - 3))
                        for c in (2 * u, 2 * u + 1):
                            mm = three(pe, ps[:, FOLD_BANK[n % 4], (c % 2) * 256:(c % 2) * 256 + 256],
                                       [a[:, j, c * P:(c + 1) * P] for a in wk],
                                       [a[:, :, :].rearrange("p h (b q) -> p b h q", b=GB) for a in qz[j % 2]], True, True)
                        mm.then_inc(fold_ready.sem, 1)
                pe.wait_ge(fold_lo.sem, fold_lo.at(t, 2 * PAIRS))
                pe.wait_ge(o_lo_done.sem, o_lo_done.at(t, 0))
                for b in range(GB + 1):
                    if b > 0:
                        turn_probs(b - 1)
                    if b < GB:
                        scores(b)
                    if b > 0:
                        mix(b - 1)
                pe.wait_ge(v_loaded.sem, v_loaded.at(t, 48))
                pe.wait_ge(last_copy.sem, last_copy.at(t, GB))
                pe.wait_ge(last_lo.sem, last_lo.at(t, GB))
                pe.wait_ge(mixed_lo.sem, mixed_lo.at(t, GB * DC))
                for j in range(PAIRS):
                    if j >= 4:
                        pe.wait_ge(o_lo_done.sem, o_lo_done.at(t, 2 * (j - 3)))
                    out = ps[:, O_BANK[j % 4], 0:2 * P]
                    for c in range(DC):
                        three(pe, out, [a[:, c, j * P:(j + 1) * P] for a in w_v],
                              [a[:, c, :, 2 * j * SQ:2 * (j + 1) * SQ].rearrange("p b (h q) -> p h b q", h=2) for a in fold], c == 0, False)
                    pe.matmul(out, last_v[:, j * P:(j + 1) * P],
                              last_p[:, 2 * j:2 * j + 2, :, :].rearrange("p h b q -> p h (b q)"),
                              start=False, stop=True).then_inc(o_ready.sem, 1)

        @block.vector
        def _(dve):
            dve.sem_inc(o_lo_done.sem, 1)
            with dve.Fori(0, TURNS) as t:
                for n in range(2 * PAIRS):
                    j, u = divmod(n, 2)
                    dve.wait_ge(fold_hi.sem, fold_hi.at(t, n + 1))
                    hi, lo = (pair_of_heads(a, j, u) for a in fold)
                    dve.tensor_tensor(lo, ps[:, FOLD_BANK[n % 4], :].rearrange("p (c n) -> p c n", n=2 * SQ), f32(hi),
                                      ALU.subtract).then_inc(fold_lo.sem, 1)

                def softmax(b):
                    for i in range(TILES):
                        dve.wait_ge(scores_ready.sem, scores_ready.at(t, b * TILES + i + 1))
                        dve.tensor_reduce(negmax[:, i:i + 1], ps[:, S_BANK[i], 0:SK], AX_X, ALU.max, negate=True)\
                            .then_inc(max_done.sem, 1)
                    dve.wait_ge(exp_done.sem, exp_done.at(t, (b + 1) * TILES))
                    dve.reciprocal(share[:, :], total[:, :]).then_inc(share_done.sem, 1)
                    dve.wait_ge(share_done.sem, share_done.at(t, b + 1))
                    dve.tensor_tensor(last_z[:, b, :, b], prob[:, :, SK - 1], share[:, :], ALU.mult)
                    for i in range(TILES):
                        last = dve.tensor_scalar(prob[:, i, 0:KT * P], prob[:, i, 0:KT * P], share[:, i:i + 1], None,
                                                 ALU.mult)
                    last.then_inc(probs_ready.sem, 1)

                def split_probs(b):
                    for k in range(KT):
                        dve.wait_ge(pT_hi.sem, pT_hi.at(t, b * KT + k + 1))
                        dve.tensor_tensor(pT[1][:, k, :], ps[:, T_BANK[k], :], f32(pT[0][:, k, :]), ALU.subtract)\
                            .then_inc(pT_lo.sem, 1)
                    dve.wait_ge(last_hi.sem, last_hi.at(t, b + 1))
                    dve.wait_ge(last_copy.sem, last_copy.at(t, b + 1))
                    dve.tensor_tensor(last_p[64:64 + GB, :, b, :],
                                      ps[0:GB, L_BANK, :].rearrange("p (h q) -> p h q", q=SQ),
                                      f32(last_p[0:GB, :, b, :]), ALU.subtract).then_inc(last_lo.sem, 1)

                def split_mixed(b):
                    for c in range(DC):
                        dve.wait_ge(mixed_hi.sem, mixed_hi.at(t, b * DC + c + 1))
                        dve.tensor_tensor(fold[1][:, c, b, :], ps[:, M_BANK[c % 2], :], f32(fold[0][:, c, b, :]),
                                          ALU.subtract)\
                            .then_inc(mixed_lo.sem, 1)

                for b in range(GB + 1):
                    if b > 0:
                        split_probs(b - 1)
                    if b < GB:
                        softmax(b)
                    if b > 0:
                        split_mixed(b - 1)
                for j in range(PAIRS):
                    dve.wait_ge(o_hi_done.sem, o_hi_done.at(t, 2 * j + 2))
                    for h in range(2):
                        r = slice(h * HE, (h + 1) * HE)
                        dve.tensor_tensor(o[1][r, j, :], ps[r, O_BANK[j % 4], h * P:(h + 1) * P],
                                          f32(o[0][r, j, :]), ALU.subtract).then_inc(o_lo_done.sem, 1)

        @block.scalar
        def _(act):
            with act.Fori(0, TURNS) as t:
                def split_T(b):
                    act.wait_ge(T_loaded.sem, T_loaded.at(t, 16 * (b + 1)))
                    act.wait_ge(scores_ready.sem, scores_ready.at(t, (b - 1) * TILES))
                    act.activation(cT[b % 2][0][:, :, 0:SK], raw_T[:, :, :], ACT.Copy).then_inc(Thi_done.sem, 1)

                def split_n(b):
                    act.wait_ge(n_loaded.sem, n_loaded.at(t, 16 * (b + 1)))
                    act.wait_ge(mixed.sem, mixed.at(t, (b - 1) * DC))
                    act.activation(cn[b % 2][0][:, :, :], raw_n[:, :, :], ACT.Copy).then_inc(nhi_done.sem, 1)

                for n in range(2 * PAIRS):
                    if n == 8:
                        split_T(0)
                        split_n(0)
                    j, u = divmod(n, 2)
                    act.wait_ge(fold_ready.sem, fold_ready.at(t, n + 1))
                    act.activation(pair_of_heads(fold[0], j, u),
                                   ps[:, FOLD_BANK[n % 4], :].rearrange("p (c n) -> p c n", n=2 * SQ), ACT.Copy)\
                        .then_inc(fold_hi.sem, 1)
                split_T(1)
                split_n(1)
                for b in range(GB + 1):
                    if b > 0:
                        for k in range(KT):
                            act.wait_ge(turned.sem, turned.at(t, (b - 1) * KT + k + 1))
                            act.activation(pT[0][:, k, :], ps[:, T_BANK[k], :], ACT.Copy).then_inc(pT_hi.sem, 1)
                        act.wait_ge(last_turned.sem, last_turned.at(t, b))
                        row = ps[0:GB, L_BANK, :].rearrange("p (h q) -> p h q", q=SQ)
                        act.activation(last_p[0:GB, :, b - 1, :], row, ACT.Copy).then_inc(last_hi.sem, 1)
                        act.activation(last_p[32:32 + GB, :, b - 1, :], row, ACT.Copy).then_inc(last_copy.sem, 1)
                    if 0 < b < GB - 1:
                        split_T(b + 1)
                    if b < GB:
                        for i in range(TILES):
                            act.wait_ge(max_done.sem, max_done.at(t, b * TILES + i + 1))
                            act.activation(prob[:, i, 0:SK], ps[:, S_BANK[i], 0:SK], ACT.Exp,
                                           bias=negmax[:, i:i + 1], accum_out=total[:, i:i + 1])\
                                .then_inc(exp_done.sem, 1)
                    if b > 0:
                        for c in range(DC):
                            act.wait_ge(mixed.sem, mixed.at(t, (b - 1) * DC + c + 1))
                            act.activation(fold[0][:, c, b - 1, :], ps[:, M_BANK[c % 2], :], ACT.Copy)\
                                .then_inc(mixed_hi.sem, 1)
                        if b + 1 < GB:
                            split_n(b + 1)
                for j in range(PAIRS):
                    act.wait_ge(o_ready.sem, o_ready.at(t, j + 1))
                    if j == 0:
                        act.wait_ge(o_free.sem, o_free.at(t, 0))
                    for h in range(2):
                        r = slice(h * HE, (h + 1) * HE)
                        act.activation(o[0][r, j, :], ps[r, O_BANK[j % 4], h * P:(h + 1) * P], ACT.Copy)\
                            .then_inc(o_hi_done.sem, 1)


def last_values(nc, last_T, w_v, v_hi, v_lo):
    dim, B = last_T.shape
    DC, inner = w_v[0].shape[1], w_v[0].shape[2]
    with ExitStack() as ctx:
        s = Scope(nc, ctx, "v")
        lT = s.pair("lT", [P, DC, B])
        raw = s.sb("raw", [P, DC, B])
        v = s.pair("v", [B, inner])
        ps = s.psum()
        loaded, hi_done, lo_done, ready = s.sem("loaded"), s.sem("hi_done"), s.sem("lo_done"), s.sem("ready")
        vhi_done, vlo_done, stored = s.sem("vhi_done"), s.sem("vlo_done"), s.sem("stored")
        block = ctx.enter_context(nc.Block())
        acc = ps[0:B, 0:2, :]

        @block.sync
        def _(sp):
            sp.dma_start(raw[:, :, :], last_T.rearrange("(c p) b -> p c b", p=P)).then_inc(loaded, 16)
            sp.wait_ge(vhi_done, 1)
            sp.dma_start(v_hi, f32(v[0][:, :])).then_inc(stored, 16)
            sp.wait_ge(vlo_done, 1)
            sp.dma_start(v_lo, f32(v[1][:, :])).then_inc(stored, 16)
            sp.wait_ge(stored, 32)

        @block.scalar
        def _(act):
            act.wait_ge(loaded, 16)
            act.activation(lT[0][:, :, :], raw[:, :, :], ACT.Copy).then_inc(hi_done, 1)
            act.wait_ge(ready, 2)
            act.activation(v[0][:, :].rearrange("p (h n) -> p h n", h=2), acc, ACT.Copy).then_inc(vhi_done, 1)

        @block.vector
        def _(dve):
            dve.wait_ge(hi_done, 1)
            dve.tensor_tensor(lT[1][:, :, :], raw[:, :, :], f32(lT[0][:, :, :]), ALU.subtract).then_inc(lo_done, 1)
            dve.wait_ge(vhi_done, 1)
            dve.tensor_tensor(v[1][:, :].rearrange("p (h n) -> p h n", h=2), acc,
                              f32(v[0][:, :]).rearrange("p (h n) -> p h n", h=2), ALU.subtract).then_inc(vlo_done, 1)

        @block.tensor
        def _(pe):
            pe.wait_ge(lo_done, 1)
            for h in range(2):
                for c in range(DC):
                    mm = three(pe, ps[0:B, h, :], [a[:, c, :] for a in lT],
                               [a[:, c, h * 512:(h + 1) * 512] for a in w_v], c == 0, c == DC - 1)
                mm.then_inc(ready, 1)


def head_attention(nc, x, out_w, bias, gate, wqkv, o_hi, o_lo, qkv, mixed_dram, x2, identity, block_mask):
    tokens, dim = x.shape
    PAIRS, DC, TT = out_w.shape[0] // P, dim // P, 4
    TURNS = tokens // (TT * P)
    H, HD = 16, dim // 16
    GT = P // H
    GROUPS = P // GT
    with ExitStack() as ctx:
        s = Scope(nc, ctx, "a")
        wo = s.pair("wo", [P, PAIRS * dim])
        w3 = [s.pair(f"w{k}", [P, DC * dim]) for k in range(3)]
        pieces = []
        for src, dst in [(out_w, wo)] + list(zip(wqkv, w3)):
            v = src.rearrange("(c p) n -> c p n", p=P)
            pieces += [(v[c], dst[0][:, c * dim:(c + 1) * dim], dst[1][:, c * dim:(c + 1) * dim])
                       for c in range(v.shape[0])]
        load_split(nc, "aw", pieces, dim)
        wo = [a[:, :].rearrange("p (j n) -> p j n", j=PAIRS) for a in wo]
        w3 = [[a[:, :].rearrange("p (c n) -> p c n", c=DC) for a in w] for w in w3]

        oT = [s.pair(f"oT{i}", [P, PAIRS, P]) for i in range(2)]
        xin = [s.sb(f"xin{i}", [P, dim]) for i in range(2)]
        x1 = [s.sb(f"x1{i}", [P, dim]) for i in range(3)]
        y, xn, xo, x2o = s.sb("y", [P, dim]), s.sb("xn", [P, 1, dim]), s.sb("xo", [P, dim]), s.sb("x2o", [P, dim])
        xT = s.pair("xT", [P, DC * P])
        qs, ks, vs = s.sb("qs", [P, dim]), s.sb("ks", [P, dim]), s.sb("vs", [P, dim])
        qmax, kmax = s.sb("qmax", [P, H]), s.sb("kmax", [P, HD])
        sums, inv = s.sb("sums", [P, H + HD]), s.sb("inv", [P, H + HD])
        rows = [s.sb(f"rows{k}", [P, GROUPS, HD]) for k in range(3)]
        qT, kT = s.sb("qT", [P, 4, P]), s.sb("kT", [P, 4, P])
        weights = s.sb("weights", [P, 4, 4 * P])
        od = s.sb("od", [P, GROUPS, HD])
        bias_b, gate_b, tanh_b = s.sb("bias", [P, dim]), s.sb("gate", [P, 1]), s.sb("tanh", [P, 1])
        mask, ident = s.sb("mask", [P, P]), s.sb("ident", [P, P])
        stats, moments = s.sb("stats", [P, 1, 6]), s.sb("moments", [P, 1, 2])
        shifted, rstd, power = s.sb("shifted", [P, 1]), s.sb("rstd", [P, 1]), s.sb("power", [P, 1])
        ps = s.psum()
        Y, V, XT, OUT, Q, K, W = 0, 0, 1, 1, 2, 3, 4

        once, power_set, tanh_done = s.sem("once"), s.sem("power_set"), s.sem("tanh_done")
        in_loaded = [s.count(f"in_loaded{i}", 48 * TT // 2) for i in range(2)]
        DVE_STEPS = 6 * TT
        chain_sem = s.sem("dve_chain")
        y_ready, y_free = s.count("y_ready", TT, 2), s.count("y_free", TT)
        x1_done = s.count("x1_done", TT, 2)
        var_ready, rstd_done = s.count("var_ready", TT), s.count("rstd_done", TT)
        normed = s.count("normed", TT)
        x_turned, xhi_done, xlo_done = s.count("x_turned", TT), s.count("xhi_done", TT), s.count("xlo_done", TT)
        q_ready, k_ready, v_ready = s.count("q_ready", TT), s.count("k_ready", TT), s.count("v_ready", TT)
        q_shift, k_shift = s.count("q_shift", TT), s.count("k_shift", TT)
        q_exp, k_exp = s.count("q_exp", TT), s.count("k_exp", TT)
        q_done, k_done = s.count("q_done", TT), s.count("k_done", TT)
        v_done = s.count("v_done", TT, 1)
        q_written = s.count("q_written", 48 * TT, 48)
        rows_read = s.count("rows_read", 48 * TT)
        q_turned, k_turned = s.count("q_turned", TT), s.count("k_turned", TT)
        qT_done, kT_done = s.count("qT_done", TT), s.count("kT_done", TT)
        dots_ready, masked = s.count("dots_ready", 4 * TT), s.count("masked", 4 * TT)
        out_ready, out_done = s.count("out_ready", TT, 1), s.count("out_done", TT, 1)
        out_written, out_read = s.count("out_written", 16 * TT, 16), s.count("out_read", 16 * TT)
        x2_done, x2_stored = s.count("x2_done", TT, 1), s.count("x2_stored", 16 * TT, 16)
        block = ctx.enter_context(nc.Block())

        @block.gpsimd
        def _(pool):
            pool.memset(power[:, :], -0.5).then_inc(power_set, 1)
            pool.wait_ge(power_set, 1)
            with pool.Fori(0, TURNS) as t:
                for i in range(TT):
                    n = t * (TT * P) + i * P
                    pool.wait_ge(y_ready.sem, y_ready.at(t, i - 1))
                    pool.wait_ge(x1_done.sem, x1_done.at(t, i - 1))
                    for dst, src in zip(oT[i % 2], (o_hi, o_lo)):
                        pool.dma_start(f32(dst[:, :, :]), src[:, :, bass.ds(n, P)].rearrange("j p n -> p j n"))\
                            .then_inc(in_loaded[i % 2].sem, 16)
                    pool.dma_start(xin[i % 2][:, :], x[bass.ds(n, P), :]).then_inc(in_loaded[i % 2].sem, 16)
                    if i > 0:
                        pool.wait_ge(var_ready.sem, var_ready.at(t, i))
                        pool.tensor_tensor(rstd[:, :], shifted[:, :], power[:, :], ALU.pow).then_inc(rstd_done.sem, 1)
                pool.wait_ge(var_ready.sem, var_ready.at(t, TT))
                pool.tensor_tensor(rstd[:, :], shifted[:, :], power[:, :], ALU.pow).then_inc(rstd_done.sem, 1)

        @block.sync
        def _(sp):
            for dst, src in ((ident[:, :], identity), (mask[:, :], block_mask),
                             (bias_b[:, :], bias.partition_broadcast(P)), (gate_b[:, :], gate.partition_broadcast(P))):
                sp.dma_start(dst, src).then_inc(once, 16)
            with sp.Fori(0, TURNS) as t:
                def turned_rows(ap, i):
                    return ap[bass.ds(t * (TT * P) + i * P, P), :]\
                        .rearrange("(g t) (h e) -> (t h) g e", t=GT, h=H)

                for i in range(TT + 2):
                    if i > 1:
                        sp.wait_ge(x2_done.sem, x2_done.at(t, i - 1))
                        sp.dma_start(x2[bass.ds(t * (TT * P) + (i - 2) * P, P), :], x2o[:, :])\
                            .then_inc(x2_stored.sem, 16)
                    if i < TT:
                        for k, (src, done) in enumerate(((vs, v_done), (ks, k_done), (qs, q_done))):
                            sp.wait_ge(done.sem, done.at(t, i + 1))
                            sp.dma_start(qkv[k, bass.ds(t * (TT * P) + i * P, P), :], src[:, :])\
                                .then_inc(q_written.sem, 16)
                        sp.wait_ge(q_written.sem, q_written.at(t, 48 * (i + 1)))
                        sp.wait_ge(out_ready.sem, out_ready.at(t, i))
                        for k in range(3):
                            sp.dma_start(rows[k][:, :, :], turned_rows(qkv[k], i)).then_inc(rows_read.sem, 16)
                    if 0 < i <= TT:
                        sp.wait_ge(out_done.sem, out_done.at(t, i))
                        sp.dma_start(turned_rows(mixed_dram, i - 1), od[:, :, :]).then_inc(out_written.sem, 16)
                        sp.wait_ge(out_written.sem, out_written.at(t, 16 * i))
                        sp.wait_ge(x2_done.sem, x2_done.at(t, i - 1))
                        sp.dma_start(xo[:, :], mixed_dram[bass.ds(t * (TT * P) + (i - 1) * P, P), :])\
                            .then_inc(out_read.sem, 16)
            sp.wait_ge(x2_stored.sem, 16 + TURNS * x2_stored.per)

        @block.tensor
        def _(pe):
            pe.sem_inc(y_ready.sem, 2)
            pe.sem_inc(out_ready.sem, 1)
            pe.wait_ge(once, 64)
            with pe.Fori(0, TURNS) as t:
                for i in range(TT + 1):
                    if i < TT:
                        pe.wait_ge(in_loaded[i % 2].sem, in_loaded[i % 2].at(t, 48 * (i // 2 + 1)))
                        pe.wait_ge(v_done.sem, v_done.at(t, i))
                        for j in range(PAIRS):
                            mm = three(pe, ps[:, Y, :], [a[:, j, :] for a in oT[i % 2]], [a[:, j, :] for a in wo],
                                       j == 0, j == PAIRS - 1)
                        mm.then_inc(y_ready.sem, 1)
                    if i > 0:
                        pe.wait_ge(rows_read.sem, rows_read.at(t, 48 * i))
                        for k, bank, done in ((0, K, k_turned), (1, Q, q_turned)):
                            for u in range(4):
                                mm = pe.transpose(ps[:, bank, u * P:(u + 1) * P],
                                                  rows[1 if k == 0 else 2][:, 4 * u:4 * u + 4, :]
                                                  .rearrange("p g e -> p (g e)"), ident[:, :])
                            mm.then_inc(done.sem, 1)
                    if i < TT:
                        pe.wait_ge(normed.sem, normed.at(t, i + 1))
                        pe.wait_ge(out_done.sem, out_done.at(t, max(i - 1, 0)))
                        for c in range(DC):
                            mm = pe.transpose(ps[:, XT, c * P:(c + 1) * P], xn[:, 0, c * P:(c + 1) * P], ident[:, :])
                        mm.then_inc(x_turned.sem, 1)
                    if i > 0:
                        pe.wait_ge(qT_done.sem, qT_done.at(t, i))
                        pe.wait_ge(kT_done.sem, kT_done.at(t, i))
                        for r in range(4):
                            g = slice(r * HD, (r + 1) * HD)
                            for u in range(4):
                                mm = pe.matmul(ps[:, W + r, u * P:(u + 1) * P], kT[g, u, :], qT[g, u, :],
                                               start=True, stop=True)
                            mm.then_inc(dots_ready.sem, 1)
                    if i < TT:
                        pe.wait_ge(xlo_done.sem, xlo_done.at(t, i + 1))
                        for k, bank, done in ((1, K, k_ready), (0, Q, q_ready), (2, V, v_ready)):
                            if k == 2:
                                pe.wait_ge(y_free.sem, y_free.at(t, i + 1))
                            for c in range(DC):
                                mm = three(pe, ps[:, bank, :], [a[:, c * P:(c + 1) * P] for a in xT],
                                           [a[:, c, :] for a in w3[k]], c == 0, c == DC - 1)
                            mm.then_inc(done.sem, 1)
                    if i > 0:
                        pe.wait_ge(masked.sem, masked.at(t, 4 * i))
                        for g in range(GROUPS):
                            u, r = divmod(g, 4)
                            mm = pe.matmul(ps[:, OUT, g * HD:(g + 1) * HD], weights[:, r, u * P:(u + 1) * P],
                                           rows[0][:, g, :], start=True, stop=True)
                        mm.then_inc(out_ready.sem, 1)

        @block.scalar
        def _(act):
            act.sem_inc(v_done.sem, 1)
            act.sem_inc(out_done.sem, 1)
            act.sem_inc(q_written.sem, 48)
            act.sem_inc(out_written.sem, 16)
            act.sem_inc(x2_stored.sem, 16)
            act.wait_ge(once, 64)
            act.activation(tanh_b[:, :], gate_b[:, :], ACT.Tanh).then_inc(tanh_done, 1)
            with act.Fori(0, TURNS) as t:
                for i in range(TT + 1):
                    if i > 0:
                        act.wait_ge(q_turned.sem, q_turned.at(t, i))
                        act.activation(qT[:, :, :], ps[:, Q, :].rearrange("p (u n) -> p u n", u=4), ACT.Copy)\
                            .then_inc(qT_done.sem, 1)
                    if i < TT:
                        act.wait_ge(x_turned.sem, x_turned.at(t, i + 1))
                        act.activation(xT[0][:, :], ps[:, XT, :], ACT.Copy).then_inc(xhi_done.sem, 1)
                        for src, shift, done in ((ks, k_shift, k_exp), (qs, q_shift, q_exp)):
                            act.wait_ge(shift.sem, shift.at(t, i + 1))
                            act.activation(src[:, :], src[:, :], ACT.Exp).then_inc(done.sem, 1)
                        act.wait_ge(v_ready.sem, v_ready.at(t, i + 1))
                        act.wait_ge(q_written.sem, q_written.at(t, 48 * i))
                        act.activation(vs[:, :], ps[:, V, :], ACT.Copy).then_inc(v_done.sem, 1)
                    if i > 0:
                        act.wait_ge(out_ready.sem, out_ready.at(t, i))
                        act.wait_ge(out_written.sem, out_written.at(t, 16 * (i - 1)))
                        act.activation(od[:, :, :], ps[:, OUT, :].rearrange("p (g e) -> p g e", g=GROUPS), ACT.Copy)\
                            .then_inc(out_done.sem, 1)

        @block.vector
        def _(dve):
            dve.sem_inc(x1_done.sem, 2)
            dve.sem_inc(x2_done.sem, 1)
            dve.wait_ge(once, 64)
            dve.wait_ge(tanh_done, 1)
            heads_last = "p (h e) -> p e h"
            with dve.Fori(0, TURNS) as t:
                chain = Chain(dve, chain_sem, t, DVE_STEPS)
                for i in range(TT + 2):
                    if i < TT:
                        dve.wait_ge(y_ready.sem, y_ready.at(t, i + 1))
                        ins = dve.tensor_tensor(y[:, :], ps[:, Y, :], bias_b[:, :], ALU.add)
                        ins.then_inc(y_free.sem, 1)
                        dve.wait_ge(y_free.sem, y_free.at(t, i + 1))
                        dve.wait_ge(in_loaded[i % 2].sem, in_loaded[i % 2].at(t, 48 * (i // 2 + 1)))
                        here = x1[i % 3]
                        dve.scalar_tensor_tensor(here[:, :], y[:, :], tanh_b[:, 0:1], xin[i % 2][:, :], ALU.mult,
                                                 ALU.add).then_inc(x1_done.sem, 1)
                        dve.wait_ge(x1_done.sem, x1_done.at(t, i + 1))
                        src = here[:, :].rearrange("p (i d) -> p i d", i=1)
                        norm_moments(dve, chain, src, stats, moments, shifted, 1, var_ready)
                        dve.wait_ge(rstd_done.sem, rstd_done.at(t, i + 1))
                        norm_scale(dve, xn, src, moments, rstd, 1).then_inc(normed.sem, 1)
                    if 0 < i <= TT:
                        dve.wait_ge(k_turned.sem, k_turned.at(t, i))
                        dve.tensor_copy(kT[:, :, :], ps[:, K, :].rearrange("p (u n) -> p u n", u=4))\
                            .then_inc(kT_done.sem, 1)
                    if i < TT:
                        dve.wait_ge(xhi_done.sem, xhi_done.at(t, i + 1))
                        dve.tensor_tensor(xT[1][:, :], ps[:, XT, :], f32(xT[0][:, :]), ALU.subtract)\
                            .then_inc(xlo_done.sem, 1)
                    if 0 < i <= TT:
                        for r in range(4):
                            dve.wait_ge(dots_ready.sem, dots_ready.at(t, 4 * (i - 1) + r + 1))
                            dve.tensor_tensor(weights[:, r, :].rearrange("p (u n) -> p u n", u=4),
                                              ps[:, W + r, :].rearrange("p (u n) -> p u n", u=4),
                                              mask[:, :].rearrange("p (u n) -> p u n", u=1).to_broadcast([P, 4, P]),
                                              ALU.mult).then_inc(masked.sem, 1)
                    if i < TT:
                        dve.wait_ge(q_written.sem, q_written.at(t, 48 * i))
                        dve.wait_ge(k_ready.sem, k_ready.at(t, i + 1))
                        chain.step(dve.tensor_reduce(kmax[:, :], ps[:, K, :].rearrange(heads_last, h=H), AX_X, ALU.max))
                        dve.tensor_tensor(ks[:, :].rearrange("p (h e) -> p h e", h=H),
                                          ps[:, K, :].rearrange("p (h e) -> p h e", h=H),
                                          kmax[:, :].rearrange("p (h e) -> p h e", h=1).to_broadcast([P, H, HD]),
                                          ALU.subtract).then_inc(k_shift.sem, 1)
                        dve.wait_ge(q_ready.sem, q_ready.at(t, i + 1))
                        chain.step(dve.tensor_reduce(qmax[:, :], ps[:, Q, :].rearrange("p (h e) -> p h e", h=H), AX_X,
                                                     ALU.max))
                        dve.tensor_tensor(qs[:, :].rearrange("p (h e) -> p h e", h=H),
                                          ps[:, Q, :].rearrange("p (h e) -> p h e", h=H),
                                          qmax[:, :].rearrange("p (h e) -> p h e", e=1).to_broadcast([P, H, HD]),
                                          ALU.subtract).then_inc(q_shift.sem, 1)
                        dve.wait_ge(k_exp.sem, k_exp.at(t, i + 1))
                        dve.tensor_reduce(sums[:, H:], ks[:, :].rearrange(heads_last, h=H), AX_X, ALU.add)
                        dve.wait_ge(q_exp.sem, q_exp.at(t, i + 1))
                        chain.step(dve.tensor_reduce(sums[:, 0:H], qs[:, :].rearrange("p (h e) -> p h e", h=H), AX_X,
                                                     ALU.add))
                        chain.step(dve.reciprocal(inv[:, :], sums[:, :]))
                        dve.tensor_tensor(ks[:, :].rearrange("p (h e) -> p h e", h=H),
                                          ks[:, :].rearrange("p (h e) -> p h e", h=H),
                                          inv[:, H:].rearrange("p (h e) -> p h e", h=1).to_broadcast([P, H, HD]),
                                          ALU.mult).then_inc(k_done.sem, 1)
                        dve.tensor_tensor(qs[:, :].rearrange("p (h e) -> p h e", h=H),
                                          qs[:, :].rearrange("p (h e) -> p h e", h=H),
                                          inv[:, 0:H].rearrange("p (h e) -> p h e", e=1).to_broadcast([P, H, HD]),
                                          ALU.mult).then_inc(q_done.sem, 1)
                    if i > 1:
                        dve.wait_ge(out_read.sem, out_read.at(t, 16 * (i - 1)))
                        dve.wait_ge(x2_stored.sem, x2_stored.at(t, 16 * (i - 2)))
                        dve.tensor_tensor(x2o[:, :], x1[(i - 2) % 3][:, :], xo[:, :], ALU.add).then_inc(x2_done.sem, 1)
                assert chain.n == DVE_STEPS


def gated_mlp(nc, x2, wg, wu, wd, out, identity, scale):
    tokens, dim = x2.shape
    hidden = wg.shape[1]
    DC, HC, TT = dim // P, hidden // P, 4
    N = TT * P
    TURNS = tokens // N
    with ExitStack() as ctx:
        s = Scope(nc, ctx, "f")
        w_g, w_u, w_d = s.pair("wg", [P, DC * hidden]), s.pair("wu", [P, DC * hidden]), s.pair("wd", [P, HC * dim])
        pieces = []
        width = dim
        for src, dst in ((wg, w_g), (wu, w_u), (wd, w_d)):
            v = src.rearrange("(c p) n -> c p n", p=P)
            n = v.shape[2]
            for c in range(v.shape[0]):
                for a in range(0, n, width):
                    b = c * n + a
                    pieces.append((v[c, :, a:a + width], dst[0][:, b:b + width], dst[1][:, b:b + width]))
        load_split(nc, "fw", pieces, width, mybir.dt.int32, scale)
        w_g, w_u = ([a[:, :].rearrange("p (c n) -> p c n", c=DC) for a in w] for w in (w_g, w_u))
        w_d = [a[:, :].rearrange("p (c n) -> p c n", c=HC) for a in w_d]

        xin, xn = s.sb("xin", [P, TT, dim]), s.sb("xn", [P, TT, dim])
        xT = s.pair("xT", [P, DC, N])
        sig, gated, h32 = s.sb("sig", [P, N]), s.sb("gated", [P, N]), s.sb("h32", [P, N])
        h = [s.pair(f"h{i}", [P, N]) for i in range(2)]
        stats, moments = s.sb("stats", [P, TT, 6]), s.sb("moments", [P, TT, 2])
        shifted, rstd, power = s.sb("shifted", [P, TT]), s.sb("rstd", [P, TT]), s.sb("power", [P, TT])
        ident = s.sb("ident", [P, P])
        ps = s.psum()
        once, power_set = s.sem("once"), s.sem("power_set")
        x_loaded, stored = s.count("x_loaded", 16), s.count("stored", 16, 16)
        chain_sem = s.sem("dve_chain")
        DVE_STEPS = 2
        var_ready, rstd_done, normed = s.count("var_ready", 1), s.count("rstd_done", 1), s.count("normed", 1)
        turned, xhi_done, xlo_done = s.count("turned", DC), s.count("xhi_done", DC), s.count("xlo_done", DC)
        gate_ready, up_ready = s.count("gate_ready", HC), s.count("up_ready", HC)
        sig_done, gated_done = s.count("sig_done", HC), s.count("gated_done", HC)
        h_done, hhi_done, hlo_done = s.count("h_done", HC), s.count("hhi_done", HC), s.count("hlo_done", HC)
        down_done = s.count("down_done", HC - 1)
        y_ready, y_done = s.count("y_ready", 1), s.count("y_done", 1, 1)
        block = ctx.enter_context(nc.Block())

        @block.sync
        def _(sp):
            sp.dma_start(ident[:, :], identity).then_inc(once, 16)
            with sp.Fori(0, TURNS) as t:
                sp.wait_ge(stored.sem, stored.at(t, 0))
                sp.dma_start(xin[:, :, :], x2[bass.ds(t * N, N), :].rearrange("(i p) d -> p i d", p=P))\
                    .then_inc(x_loaded.sem, 16)
                sp.wait_ge(y_done.sem, y_done.at(t, 1))
                sp.dma_start(out[bass.ds(t * N, N), :].rearrange("(i p) d -> p i d", p=P), xn[:, :, :])\
                    .then_inc(stored.sem, 16)
            sp.wait_ge(stored.sem, 16 + 16 * TURNS)

        @block.gpsimd
        def _(pool):
            pool.memset(power[:, :], -0.5).then_inc(power_set, 1)
            pool.wait_ge(power_set, 1)
            with pool.Fori(0, TURNS) as t:
                pool.wait_ge(var_ready.sem, var_ready.at(t, 1))
                pool.tensor_tensor(rstd[:, :], shifted[:, :], power[:, :], ALU.pow).then_inc(rstd_done.sem, 1)

        @block.vector
        def _(dve):
            dve.sem_inc(y_done.sem, 1)
            with dve.Fori(0, TURNS) as t:
                chain = Chain(dve, chain_sem, t, DVE_STEPS)
                dve.wait_ge(x_loaded.sem, x_loaded.at(t, 16))
                norm_moments(dve, chain, xin, stats, moments, shifted, TT, var_ready)
                dve.wait_ge(rstd_done.sem, rstd_done.at(t, 1))
                norm_scale(dve, xn, xin, moments, rstd, TT).then_inc(normed.sem, 1)
                for c in range(DC):
                    dve.wait_ge(xhi_done.sem, xhi_done.at(t, c + 1))
                    dve.tensor_tensor(xT[1][:, c, :], ps[:, c, :], f32(xT[0][:, c, :]), ALU.subtract)\
                        .then_inc(xlo_done.sem, 1)
                for k in range(HC):
                    dve.wait_ge(sig_done.sem, sig_done.at(t, k + 1))
                    dve.tensor_tensor(gated[:, :], ps[:, 4 + 2 * (k % 2), :], sig[:, :], ALU.mult)\
                        .then_inc(gated_done.sem, 1)
                    dve.wait_ge(gated_done.sem, gated_done.at(t, k + 1))
                    dve.wait_ge(up_ready.sem, up_ready.at(t, k + 1))
                    dve.tensor_tensor(h32[:, :], ps[:, 5 + 2 * (k % 2), :], gated[:, :], ALU.mult)\
                        .then_inc(h_done.sem, 1)
                    dve.wait_ge(hhi_done.sem, hhi_done.at(t, k + 1))
                    dve.tensor_tensor(h[k % 2][1][:, :], h32[:, :], f32(h[k % 2][0][:, :]), ALU.subtract)\
                        .then_inc(hlo_done.sem, 1)
                dve.wait_ge(y_ready.sem, y_ready.at(t, 1))
                dve.tensor_tensor(xn[:, :, :], ps[:, 0:TT, :], xin[:, :, :], ALU.add).then_inc(y_done.sem, 1)

        @block.scalar
        def _(act):
            act.sem_inc(stored.sem, 16)
            with act.Fori(0, TURNS) as t:
                for c in range(DC):
                    act.wait_ge(turned.sem, turned.at(t, c + 1))
                    act.activation(xT[0][:, c, :], ps[:, c, :], ACT.Copy).then_inc(xhi_done.sem, 1)
                for k in range(HC):
                    act.wait_ge(gate_ready.sem, gate_ready.at(t, k + 1))
                    if k > 0:
                        act.wait_ge(gated_done.sem, gated_done.at(t, k))
                    act.activation(sig[:, :], ps[:, 4 + 2 * (k % 2), :], ACT.Sigmoid).then_inc(sig_done.sem, 1)
                    act.wait_ge(h_done.sem, h_done.at(t, k + 1))
                    if k >= 2:
                        act.wait_ge(down_done.sem, down_done.at(t, k - 1))
                    act.activation(h[k % 2][0][:, :], h32[:, :], ACT.Copy).then_inc(hhi_done.sem, 1)

        @block.tensor
        def _(pe):
            pe.wait_ge(once, 16)
            with pe.Fori(0, TURNS) as t:
                pe.wait_ge(normed.sem, normed.at(t, 1))
                pe.wait_ge(y_done.sem, y_done.at(t, 0))
                for c in range(DC):
                    for i in range(TT):
                        mm = pe.transpose(ps[:, c, i * P:(i + 1) * P], xn[:, i, c * P:(c + 1) * P], ident[:, :])
                    mm.then_inc(turned.sem, 1)
                pe.wait_ge(xlo_done.sem, xlo_done.at(t, DC))
                for k in range(HC + 1):
                    if k < HC:
                        if k >= 2:
                            pe.wait_ge(h_done.sem, h_done.at(t, k - 1))
                        for w, bank, done in ((w_g, 4, gate_ready), (w_u, 5, up_ready)):
                            for c in range(DC):
                                mm = three(pe, ps[:, bank + 2 * (k % 2), :], [a[:, c, k * P:(k + 1) * P] for a in w],
                                           [a[:, c, :] for a in xT], c == 0, c == DC - 1)
                            mm.then_inc(done.sem, 1)
                    if k > 0:
                        pe.wait_ge(hlo_done.sem, hlo_done.at(t, k))
                        for i in range(TT):
                            mm = three(pe, ps[:, i, :], [a[:, i * P:(i + 1) * P] for a in h[(k - 1) % 2]],
                                       [a[:, k - 1, :] for a in w_d], k == 1, k == HC)
                        mm.then_inc(down_done.sem if k < HC else y_ready.sem, 1)


def build(nc, x, ctx_nat, ctx_T, last_T, gamma, beta, wq, wkT, wv, w_out, b_out, gate, aq, ak, av, wg, wu, wd,
          identity, block_mask, out):
    tokens, dim = x.shape
    inner = wq.shape[1]
    B = ctx_nat.shape[0]

    def scratch(name, shape, dt=F32):
        return nc.dram_tensor(name, shape, dt, kind="Internal").ap()

    q_hi, q_lo, o_hi, o_lo = (scratch(n, [inner // P, P, tokens]) for n in ("q_hi", "q_lo", "o_hi", "o_lo"))
    v_hi, v_lo = (scratch(n, [B, inner]) for n in ("v_hi", "v_lo"))
    qkv, mixed, x2 = scratch("qkv", [3, tokens, dim]), scratch("mixed", [tokens, dim]), scratch("x2", [tokens, dim])
    HEADS = 16
    project_queries(nc, x, gamma, beta, wq, q_hi, q_lo, identity, (inner // HEADS) ** -0.5)
    cross_attention(nc, ctx_nat, ctx_T, last_T, wkT, wv, q_hi, q_lo, v_hi, v_lo, o_hi, o_lo, identity, HEADS)
    head_attention(nc, x, w_out, b_out, gate, (aq, ak, av), o_hi, o_lo, qkv, mixed, x2, identity, block_mask)
    gated_mlp(nc, x2, wg, wu, wd, out, identity, 1.0 / 127.0)


def kernel(**inputs):
    import numpy as np
    import concourse.bacc as bacc
    from concourse.bass_utils import run_bass_kernel_spmd

    a = {k: np.asarray(v) for k, v in inputs.items()}
    B, SQ, dim = a["x"].shape
    inner = a["L0_xattn_w_q"].shape[1]
    ctx = a["ctx_1024"]
    w_kv = a["L0_xattn_w_kv"]
    heads = 16
    laid = {
        "x": a["x"].reshape(B * SQ, dim),
        "ctx_nat": ctx,
        "ctx_T": ctx.transpose(0, 2, 1),
        "last_T": ctx[:, -1, :].T,
        "gamma": a["L0_xattn_ln_gamma"].reshape(-1, P).T,
        "beta": a["L0_xattn_ln_beta"].reshape(-1, P).T,
        "wq": a["L0_xattn_w_q"],
        "wkT": w_kv[:, :inner].T,
        "wv": w_kv[:, inner:],
        "w_out": a["L0_xattn_w_out"],
        "b_out": a["L0_xattn_b_out"],
        "gate": a["L0_xattn_gate"],
        "aq": a["L0_attn_W_Q"].T,
        "ak": a["L0_attn_W_K"].T,
        "av": a["L0_attn_W_V"].T,
        "wg": a["L0_ffn_w_gate"].T,
        "wu": a["L0_ffn_w_up"].T,
        "wd": a["L0_ffn_w_down"].T,
        "identity": np.eye(P, dtype=np.float32),
        "block_mask": np.kron(np.eye(P // heads, dtype=np.float32), np.ones((heads, heads), np.float32)),
    }
    laid = {k: np.ascontiguousarray(v) for k, v in laid.items()}
    nc = bacc.Bacc("TRN2", target_bir_lowering=False, num_devices=1)
    aps = {k: nc.dram_tensor(k, v.shape, mybir.dt.from_np(v.dtype), kind="ExternalInput").ap() for k, v in laid.items()}
    out = nc.dram_tensor("out", [B * SQ, dim], F32, kind="ExternalOutput").ap()
    build(nc, out=out, **aps)
    r = run_bass_kernel_spmd(nc, [laid], core_ids=[0])
    return r.results[0]["out"].reshape(B, SQ, dim)
```

```python
from contextlib import ExitStack

import concourse.bass as bass
from concourse import mybir

ALU = mybir.AluOpType
ACT = mybir.ActivationFunctionType
F32 = mybir.dt.float32
F32R = mybir.dt.float32r
AX_X = mybir.AxisListType.X
P = 128
EPS = 1e-5


class Count:

    def __init__(self, sem, per, credit=0):
        self.sem, self.per, self.credit = sem, per, credit

    def at(self, turn, n):
        first = turn if isinstance(turn, int) else turn.min_val
        assert first * self.per + self.credit + n > 0
        return turn * self.per + (self.credit + n)


class Chain:

    def __init__(self, eng, sem, turn, per, before=0):
        self.eng, self.sem, self.turn, self.per, self.n = eng, sem, turn, per, before

    def step(self, ins):
        self.n += 1
        ins.then_inc(self.sem, 1)
        self.eng.wait_ge(self.sem, self.turn * self.per + self.n)


class Scope:

    def __init__(self, nc, ctx, name):
        self.nc, self.ctx, self.name = nc, ctx, name

    def sb(self, name, shape, dt=F32):
        return self.ctx.enter_context(self.nc.sbuf_tensor(f"{self.name}_{name}", shape, dt))

    def pair(self, name, shape):
        return self.sb(name + "_hi", shape, F32R), self.sb(name + "_lo", shape, F32R)

    def psum(self):
        return self.ctx.enter_context(self.nc.psum_tensor(f"{self.name}_ps", [P, 8, 512], F32))

    def sem(self, name):
        return self.ctx.enter_context(self.nc.semaphore(f"{self.name}_{name}"))

    def count(self, name, per, credit=0):
        return Count(self.sem(name), per, credit)


def f32(ap):
    return ap.bitcast(F32)


def three(pe, out, lhs, rhs, start, stop):
    pe.matmul(out, lhs[0], rhs[0], start=start, stop=False)
    pe.matmul(out, lhs[0], rhs[1], start=False, stop=False)
    return pe.matmul(out, lhs[1], rhs[0], start=False, stop=stop)


class WeightSplit:
    RING = 6

    def __init__(self, s, pieces, width, dt=F32, scale=1.0):
        self.pieces, self.scale = pieces, scale
        self.raw = [s.sb(f"raw{i}", [P, width], dt) for i in range(self.RING)]
        self.loaded = [s.sem(f"w_loaded{i}") for i in range(self.RING)]
        self.hi_done, self.lo_done = s.sem("w_hi_done"), s.sem("w_lo_done")

    def load(self, eng, numbers):
        for n in numbers:
            if n >= self.RING:
                eng.wait_ge(self.lo_done, n - self.RING + 1)
            eng.dma_start(self.raw[n % self.RING][:, :], self.pieces[n][0]).then_inc(self.loaded[n % self.RING], 16)

    def round(self, act, numbers):
        for n in numbers:
            act.wait_ge(self.loaded[n % self.RING], 16 * (n // self.RING + 1))
            act.activation(self.pieces[n][1], self.raw[n % self.RING][:, :], ACT.Copy, scale=self.scale)\
                .then_inc(self.hi_done, 1)

    def split(self, dve, numbers):
        for n in numbers:
            dve.wait_ge(self.loaded[n % self.RING], 16 * (n // self.RING + 1))
            dve.wait_ge(self.hi_done, n + 1)
            dve.scalar_tensor_tensor(self.pieces[n][2], self.raw[n % self.RING][:, :], self.scale,
                                     f32(self.pieces[n][1]), ALU.mult, ALU.subtract).then_inc(self.lo_done, 1)


def load_split(nc, name, pieces, width):
    with ExitStack() as ctx:
        s = Scope(nc, ctx, name)
        weights, numbers = WeightSplit(s, pieces, width), range(len(pieces))
        block = ctx.enter_context(nc.Block())

        @block.sync
        def _(sp):
            weights.load(sp, numbers)

        @block.scalar
        def _(act):
            weights.round(act, numbers)

        @block.vector
        def _(dve):
            weights.split(dve, numbers)


def norm_moments(dve, chain, src, stats, moments, shifted, tiles, asked):
    for i in range(tiles):
        ins = dve.bn_stats(stats[:, i, :], src[:, i, :])
    chain.step(ins)
    dve.memset(shifted[:, 0:tiles], EPS)
    for i in range(tiles):
        ins = dve.bn_aggr(moments[:, i, :], stats[:, i, :])
    chain.step(ins)
    dve.tensor_tensor(shifted[:, 0:tiles], shifted[:, 0:tiles], moments[:, 0:tiles, 1], ALU.add)\
        .then_inc(asked.sem, 1)


def norm_scale(dve, dst, src, moments, rstd, tiles):
    for i in range(tiles):
        ins = dve.tensor_scalar(dst[:, i, :], src[:, i, :], moments[:, i, 0:1], rstd[:, i:i + 1],
                                ALU.subtract, ALU.mult)
    return ins


def project_queries(nc, x, gamma, beta, wq, q_dram, identity, scale):
    tokens, dim = x.shape
    inner = wq.shape[1]
    DC, PAIRS, TT = dim // P, inner // P, 4
    N = TT * P
    TURNS = tokens // N
    with ExitStack() as ctx:
        s = Scope(nc, ctx, "q")
        w = s.pair("wq", [P, DC * inner])
        wsrc = wq.rearrange("(c p) n -> c p n", p=P)
        pieces = []
        for c in range(DC):
            for h in range(inner // dim):
                a = c * inner + h * dim
                pieces.append((wsrc[c, :, h * dim:(h + 1) * dim], w[0][:, a:a + dim], w[1][:, a:a + dim]))
        weights = WeightSplit(s, pieces, dim)
        wt = [t[:, :].rearrange("p (c n) -> p c n", c=DC) for t in w]

        xin, xn, xn2 = s.sb("xin", [P, TT, dim]), s.sb("xn", [P, TT, dim]), s.sb("xn2", [P, TT, dim])
        stats, moments = s.sb("stats", [P, TT, 6]), s.sb("moments", [P, TT, 2])
        shifted, rstd, power = s.sb("shifted", [P, TT]), s.sb("rstd", [P, TT]), s.sb("power", [P, TT])
        ident = s.sb("ident", [P, P])
        g, b = s.sb("gamma", [P, DC]), s.sb("beta", [P, DC])
        affine = s.sb("affine", [P, DC, N])
        xT = s.pair("xT", [P, DC, N])
        q = s.pair("q", [P, PAIRS, N])
        ps = s.psum()
        once, x_loaded, q_stored = s.sem("once"), s.count("x_loaded", 16), [s.count(f"q_stored{m}", 32, 32)
                                                                               for m in range(PAIRS // 2)]
        normed = s.count("normed", 1)
        DVE_STEPS = 5
        dve_chain = s.sem("dve_chain")
        var_ready, rstd_done, power_set = s.count("var_ready", 2), s.count("rstd_done", 2), s.sem("power_set")
        turned, affine_done = s.count("turned", DC), s.count("affine_done", DC, 0)
        xhi_done, xlo_done = s.count("xhi_done", DC), s.count("xlo_done", DC)
        q_ready, qhi_done, qlo_done = s.count("q_ready", PAIRS), s.count("qhi_done", PAIRS), s.count("qlo_done", PAIRS)
        block = ctx.enter_context(nc.Block())

        @block.sync
        def _(sp):
            sp.dma_start(ident[:, :], identity).then_inc(once, 16)
            sp.dma_start(g[:, :], gamma).then_inc(once, 16)
            sp.dma_start(b[:, :], beta).then_inc(once, 16)

            def load(tokens_of):
                sp.dma_start(xin[:, :, :], x[tokens_of, :].rearrange("(i p) d -> p i d", p=P))\
                    .then_inc(x_loaded.sem, 16)

            load(bass.ds(0, N))
            weights.load(sp, range(len(pieces)))
            with sp.Fori(0, TURNS - 1) as t:
                sp.wait_ge(normed.sem, normed.at(t, 1))
                load(bass.ds(t * N + N, N))

        @block.gpsimd
        def _(pool):
            pool.memset(power[:, :], -0.5).then_inc(power_set, 1)
            pool.wait_ge(power_set, 1)
            with pool.Fori(0, TURNS) as t:
                for k in range(2):
                    pool.wait_ge(var_ready.sem, var_ready.at(t, k + 1))
                    pool.tensor_tensor(rstd[:, :], shifted[:, :], power[:, :], ALU.pow).then_inc(rstd_done.sem, 1)

        @block.vector
        def _(dve):
            def norm_parts(t, ahead, chain):
                def first_moments():
                    dve.wait_ge(x_loaded.sem, x_loaded.at(t, 16 * (ahead + 1)))
                    norm_moments(dve, chain, xin, stats, moments, shifted, TT, var_ready)

                def first_scale():
                    dve.wait_ge(rstd_done.sem, rstd_done.at(t, 2 * ahead + 1))
                    chain.step(norm_scale(dve, xn, xin, moments, rstd, TT))

                def second_moments():
                    norm_moments(dve, chain, xn, stats, moments, shifted, TT, var_ready)

                def second_scale():
                    dve.wait_ge(rstd_done.sem, rstd_done.at(t, 2 * ahead + 2))
                    norm_scale(dve, xn2, xn, moments, rstd, TT).then_inc(normed.sem, 1)

                def affine_part(chunks):
                    for c in chunks:
                        dve.wait_ge(turned.sem, turned.at(t, DC * ahead + c + 1))
                        dve.tensor_scalar(affine[:, c, :], ps[:, c, :], g[:, c:c + 1], b[:, c:c + 1],
                                          ALU.mult, ALU.add).then_inc(affine_done.sem, 1)

                return {0: first_moments, 1: first_scale, 2: second_moments, 4: second_scale,
                        6: lambda: affine_part((0, 1)), 7: lambda: affine_part((2, 3))}

            def turn(t, parts):
                for c in range(DC):
                    dve.wait_ge(xhi_done.sem, xhi_done.at(t, c + 1))
                    dve.tensor_tensor(xT[1][:, c, :], affine[:, c, :], f32(xT[0][:, c, :]), ALU.subtract)\
                        .then_inc(xlo_done.sem, 1)
                for j in range(PAIRS):
                    dve.wait_ge(qhi_done.sem, qhi_done.at(t, j + 1))
                    dve.scalar_tensor_tensor(q[1][:, j, :], ps[:, 4 + j % 4, :], scale, f32(q[0][:, j, :]),
                                             ALU.mult, ALU.subtract).then_inc(qlo_done.sem, 1)
                    if j in parts:
                        parts[j]()

            dve.wait_ge(once, 48)
            parts = norm_parts(0, 0, Chain(dve, dve_chain, 0, DVE_STEPS))
            half = len(pieces) // 2
            for n, part in parts.items():
                part()
                if n == 0:
                    weights.split(dve, range(half))
                if n == 2:
                    weights.split(dve, range(half, len(pieces)))
            with dve.Fori(0, TURNS - 1) as t:
                chain = Chain(dve, dve_chain, t, DVE_STEPS, DVE_STEPS)
                turn(t, norm_parts(t, 1, chain))
                assert chain.n == 2 * DVE_STEPS
            turn(TURNS - 1, {})

        @block.scalar
        def _(act):
            for done in q_stored:
                act.sem_inc(done.sem, 32)
            weights.round(act, range(len(pieces)))
            with act.Fori(0, TURNS) as t:
                def store(m):
                    act.wait_ge(qhi_done.sem, qhi_done.at(t, 2 * m + 2))
                    act.wait_ge(qlo_done.sem, qlo_done.at(t, 2 * m + 2))
                    for part in range(2):
                        act.dma_start(q_dram[:, 2 * m:2 * m + 2, part, bass.ds(t * N, N)],
                                      f32(q[part][:, 2 * m:2 * m + 2, :])).then_inc(q_stored[m].sem, 16)

                for c in range(DC):
                    act.wait_ge(affine_done.sem, affine_done.at(t, c + 1))
                    act.activation(xT[0][:, c, :], affine[:, c, :], ACT.Copy).then_inc(xhi_done.sem, 1)
                for j in range(PAIRS):
                    act.wait_ge(q_ready.sem, q_ready.at(t, j + 1))
                    if j % 2 == 0:
                        act.wait_ge(q_stored[j // 2].sem, q_stored[j // 2].at(t, 0))
                    act.activation(q[0][:, j, :], ps[:, 4 + j % 4, :], ACT.Copy, scale=scale)\
                        .then_inc(qhi_done.sem, 1)
                    if j % 2 == 0 and j > 0:
                        store(j // 2 - 1)
                store(PAIRS // 2 - 1)
            for done in q_stored:
                act.wait_ge(done.sem, 32 * TURNS + 32)

        @block.tensor
        def _(pe):
            def turn_x(t, ahead):
                pe.wait_ge(normed.sem, normed.at(t, ahead + 1))
                for c in range(DC):
                    for i in range(TT):
                        mm = pe.transpose(ps[:, c, i * P:(i + 1) * P], xn2[:, i, c * P:(c + 1) * P], ident[:, :])
                    mm.then_inc(turned.sem, 1)

            def turn(t, more):
                for j in range(PAIRS):
                    if j >= 4:
                        pe.wait_ge(qlo_done.sem, qlo_done.at(t, j - 3))
                    for c in range(DC):
                        if j == 0:
                            pe.wait_ge(xlo_done.sem, xlo_done.at(t, c + 1))
                        mm = three(pe, ps[:, 4 + j % 4, :], [a[:, c, j * P:(j + 1) * P] for a in wt],
                                   [a[:, c, :] for a in xT], c == 0, c == DC - 1)
                    mm.then_inc(q_ready.sem, 1)
                    if j == PAIRS - 2 and more:
                        turn_x(t, 1)

            pe.wait_ge(once, 48)
            turn_x(0, 0)
            pe.wait_ge(weights.lo_done, len(pieces))
            with pe.Fori(0, TURNS - 1) as t:
                turn(t, True)
            turn(TURNS - 1, False)


def cross_attention(nc, ctx_nat, ctx_T, last_T, wkT, wv, q_dram, v_hi, v_lo, o_hi, o_lo, identity, heads):
    B, SK, dim = ctx_nat.shape
    inner = wv.shape[1]
    DC, PAIRS = dim // P, inner // P
    tokens = q_dram.shape[3]
    SQ = tokens // B
    GB = P // SQ
    TURNS = B // GB
    KT = SK // P
    SKE = SK + 1
    HT = P // SQ
    TILES = heads // HT
    HE = inner // heads
    assert SK == KT * P + 1 and TILES == 4 and DC == 4 and KT == 2
    with ExitStack() as ctx:
        s = Scope(nc, ctx, "x")
        wk = s.pair("wk", [P, PAIRS * dim])
        w_v = s.pair("wv", [P, DC * inner])
        wk_src, wv_src = wkT.rearrange("(j p) d -> j p d", p=P), wv.rearrange("(c p) n -> c p n", p=P)
        pieces = [(wk_src[j], wk[0][:, j * dim:(j + 1) * dim], wk[1][:, j * dim:(j + 1) * dim]) for j in range(PAIRS)]
        for c in range(DC):
            for h in range(inner // dim):
                a = c * inner + h * dim
                pieces.append((wv_src[c, :, h * dim:(h + 1) * dim], w_v[0][:, a:a + dim], w_v[1][:, a:a + dim]))
        load_split(nc, "xw", pieces, dim)
        wk = [a[:, :].rearrange("p (j d) -> p j d", j=PAIRS) for a in wk]
        w_v = [a[:, :].rearrange("p (c n) -> p c n", c=DC) for a in w_v]

        last_values(nc, last_T, w_v, v_hi, v_lo)

        fold = s.pair("fold", [P, DC, GB, heads * SQ])
        qz = [s.sb(f"qz{i}", [P, 2, 2, 2, P], F32R) for i in range(2)]
        raw_n, raw_T = s.sb("raw_n", [P, KT, dim]), s.sb("raw_T", [P, DC, SK])
        cn = [s.pair(f"cn{i}", [P, KT, dim]) for i in range(2)]
        cT = [s.pair(f"cT{i}", [P, DC, SKE]) for i in range(2)]
        prob = s.sb("prob", [P, TILES, SKE])
        pT = s.pair("pT", [P, KT, heads * SQ])
        last_p = s.sb("last_p", [P, heads, GB, SQ], F32R)
        last_v = s.sb("last_v", [P, inner], F32R)
        last_z = s.sb("last_z", [P, GB, TILES, GB])
        o = [s.pair(f"o{i}", [P, P]) for i in range(4)]
        ident = s.sb("ident", [P, P])
        negmax, total, share = s.sb("negmax", [P, TILES]), s.sb("total", [P, TILES]), s.sb("share", [P, TILES])
        ps = s.psum()
        S_BANK, T_BANK, L_BANK, M_BANK = (0, 1, 2, 5), (3, 4), 5, (6, 7)
        FOLD_BANK, O_BANK = (3, 4, 6, 7), (0, 1, 2, 5)

        once, cleared = s.sem("once"), s.sem("cleared")
        qz_loaded = [s.count(f"qz_loaded{i}", 32 * PAIRS // 4) for i in range(2)]
        v_loaded = s.count("v_loaded", 48)
        n_loaded, T_loaded = s.count("n_loaded", 16 * GB), s.count("T_loaded", 16 * GB)
        nhi_done, Thi_done = s.count("nhi_done", GB), s.count("Thi_done", GB)
        nlo_done, Tlo_done = s.count("nlo_done", GB, 1), s.count("Tlo_done", GB, 1)
        fold_ready = s.count("fold_ready", 2 * PAIRS, 8)
        fold_hi, fold_lo = s.count("fold_hi", 2 * PAIRS), s.count("fold_lo", 2 * PAIRS)
        scores_ready = s.count("scores_ready", GB * TILES, 2 * TILES)
        max_done, exp_done = s.count("max_done", GB * TILES), s.count("exp_done", GB * TILES)
        share_done, probs_ready = s.count("share_done", GB * TILES), s.count("probs_ready", GB * TILES)
        turned, last_turned = s.count("turned", GB * KT), s.count("last_turned", GB)
        pT_hi, pT_lo = s.count("pT_hi", GB * KT), s.count("pT_lo", GB * KT)
        last_hi, last_copy, last_lo = s.count("last_hi", GB), s.count("last_copy", GB), s.count("last_lo", GB)
        mixed = s.count("mixed", GB * DC, 2 * DC)
        mixed_hi, mixed_lo = s.count("mixed_hi", GB * DC), s.count("mixed_lo", GB * DC)
        o_ready = s.count("o_ready", PAIRS, 1)
        o_hi_done, o_lo_done = s.count("o_hi_done", 2 * PAIRS), s.count("o_lo_done", 2 * PAIRS, 1)
        o_stored = [s.count(f"o_stored{i}", 32 * PAIRS // 4, 32) for i in range(4)]
        SCORES_AFTER = {3: (0,), 5: (1,), 6: (2,), 7: (3,)}
        SOFTMAX_AFTER = {4: (0,), 6: (1,), 7: (2, 3)}
        block = ctx.enter_context(nc.Block())

        def pair_of_heads(a, j, u):
            return a[:, 2 * u:2 * u + 2, :, 2 * j * SQ:2 * (j + 1) * SQ].rearrange("p c b n -> p (c b) n")

        @block.sync
        def _(sp):
            sp.dma_start(ident[:, :], identity).then_inc(once, 16)
            sp.wait_ge(cleared, 1)
            with sp.Fori(0, TURNS) as t:
                def load_context(b):
                    sp.wait_ge(Tlo_done.sem, Tlo_done.at(t, b))
                    sp.dma_start(raw_T[:, :, :], ctx_T[t * GB + b].rearrange("(c p) k -> p c k", p=P))\
                        .then_inc(T_loaded.sem, 16)
                    sp.wait_ge(nlo_done.sem, nlo_done.at(t, b))
                    sp.dma_start(raw_n[:, :, :], ctx_nat[t * GB + b, 0:KT * P, :].rearrange("(k p) d -> p k d", p=P))\
                        .then_inc(n_loaded.sem, 16)

                for j in range(0, PAIRS, 2):
                    q = qz[j // 2 % 2]
                    sp.wait_ge(fold_ready.sem, fold_ready.at(t, 2 * (j - 2)))
                    for h in range(2):
                        r = slice(h * HE, (h + 1) * HE)
                        sp.dma_start(f32(q[r, :, :, h, :]), q_dram[r, j:j + 2, :, bass.ds(t * P, P)])\
                            .then_inc(qz_loaded[j // 2 % 2].sem, 16)
                    if j == 2:
                        load_context(0)
                load_context(1)
                sp.wait_ge(o_ready.sem, o_ready.at(t, 0))
                for row, src in ((0, v_hi), (32, v_lo), (64, v_hi)):
                    sp.dma_start(f32(last_v[row:row + GB, :]), src[bass.ds(t * GB, GB), :]).then_inc(v_loaded.sem, 16)
                for b in range(2, GB):
                    load_context(b)

        @block.gpsimd
        def _(pool):
            pool.memset(last_z[:, :, :, :], 0.0)
            for ap in [last_p[:, :, :, :], last_v[:, :]] + [q[:, :, :, :, :] for q in qz] +\
                      [a[:, :, SK:SKE] for c in cT for a in c]:
                last = pool.memset(f32(ap), 0.0)
            last.then_inc(cleared, 1)
            pool.sem_inc(nlo_done.sem, 1)
            pool.sem_inc(Tlo_done.sem, 1)
            with pool.Fori(0, TURNS) as t:
                for b in range(GB):
                    pool.wait_ge(Thi_done.sem, Thi_done.at(t, b + 1))
                    pool.tensor_tensor(cT[b % 2][1][:, :, 0:SK], raw_T[:, :, :], f32(cT[b % 2][0][:, :, 0:SK]),
                                       ALU.subtract).then_inc(Tlo_done.sem, 1)
                    pool.wait_ge(nhi_done.sem, nhi_done.at(t, b + 1))
                    pool.tensor_tensor(cn[b % 2][1][:, :, :], raw_n[:, :, :], f32(cn[b % 2][0][:, :, :]),
                                       ALU.subtract).then_inc(nlo_done.sem, 1)

        @block.tensor
        def _(pe):
            pe.sem_inc(fold_ready.sem, 8)
            pe.sem_inc(o_ready.sem, 1)
            pe.sem_inc(scores_ready.sem, 2 * TILES)
            pe.sem_inc(mixed.sem, 2 * DC)
            pe.wait_ge(once, 16)
            pe.wait_ge(cleared, 1)
            with pe.Fori(0, TURNS) as t:
                def fold_pair(j):
                    q = qz[j // 2 % 2]
                    if j % 2 == 0:
                        pe.wait_ge(qz_loaded[j // 2 % 2].sem, qz_loaded[j // 2 % 2].at(t, 32 * (j // 4 + 1)))
                    for u in range(2):
                        n = 2 * j + u
                        if n >= 4:
                            pe.wait_ge(fold_lo.sem, fold_lo.at(t, n - 3))
                        for c in (2 * u, 2 * u + 1):
                            mm = three(pe, ps[:, FOLD_BANK[n % 4], (c % 2) * 256:(c % 2) * 256 + 256],
                                       [a[:, j, c * P:(c + 1) * P] for a in wk],
                                       [q[:, j % 2, part].rearrange("p h (b q) -> p b h q", b=GB) for part in range(2)],
                                       True, True)
                        mm.then_inc(fold_ready.sem, 1)

                def score_tile(b, i):
                    for c in range(DC):
                        mm = three(pe, ps[:, S_BANK[i], 0:SKE],
                                   [a[:, c, b, i * P:(i + 1) * P] for a in fold],
                                   [a[:, c, :] for a in cT[b % 2]], c == 0, c == DC - 1)
                    mm.then_inc(scores_ready.sem, 1)

                def scores(b):
                    pe.wait_ge(Tlo_done.sem, Tlo_done.at(t, b + 1))
                    for i in range(TILES):
                        pe.wait_ge(exp_done.sem, exp_done.at(t, (b - 1) * TILES + i + 1))
                        if S_BANK[i] == L_BANK:
                            pe.wait_ge(last_copy.sem, last_copy.at(t, b))
                            pe.wait_ge(last_lo.sem, last_lo.at(t, b))
                        score_tile(b, i)

                def turn_probs(b):
                    for i in range(TILES):
                        pe.wait_ge(probs_ready.sem, probs_ready.at(t, b * TILES + i + 1))
                        for k in range(KT):
                            mm = pe.transpose(ps[:, T_BANK[k], i * P:(i + 1) * P], prob[:, i, k * P:(k + 1) * P],
                                              ident[:, :])
                            if i == TILES - 1:
                                mm.then_inc(turned.sem, 1)
                    for i in range(TILES):
                        mm = pe.transpose(ps[0:GB, L_BANK, i * P:(i + 1) * P], last_z[:, b, i, :], ident[:, :])
                    mm.then_inc(last_turned.sem, 1)

                def mix(b):
                    pe.wait_ge(nlo_done.sem, nlo_done.at(t, b + 1))
                    for c in range(DC):
                        if b > 0 or c >= 2:
                            pe.wait_ge(mixed_lo.sem, mixed_lo.at(t, b * DC + c - 1))
                        for k in range(KT):
                            if c == 0:
                                pe.wait_ge(pT_lo.sem, pT_lo.at(t, b * KT + k + 1))
                            mm = three(pe, ps[:, M_BANK[c % 2], :],
                                       [a[:, k, c * P:(c + 1) * P] for a in cn[b % 2]],
                                       [a[:, k, :] for a in pT], k == 0, k == KT - 1)
                        mm.then_inc(mixed.sem, 1)

                for j in range(PAIRS):
                    fold_pair(j)
                    for i in SCORES_AFTER.get(j, ()):
                        pe.wait_ge(fold_lo.sem, fold_lo.at(t, 4 * (i + 1)))
                        if i == 0:
                            pe.wait_ge(Tlo_done.sem, Tlo_done.at(t, 1))
                            pe.wait_ge(o_lo_done.sem, o_lo_done.at(t, 0))
                        score_tile(0, i)
                for b in range(1, GB + 1):
                    turn_probs(b - 1)
                    if b < GB:
                        scores(b)
                    mix(b - 1)
                for j in range(PAIRS):
                    if j >= 4:
                        pe.wait_ge(o_lo_done.sem, o_lo_done.at(t, 2 * (j - 3)))
                    out = ps[:, O_BANK[j % 4], 0:2 * P]
                    for c in range(DC):
                        if j == 0:
                            pe.wait_ge(mixed_lo.sem, mixed_lo.at(t, (GB - 1) * DC + c + 1))
                        three(pe, out, [a[:, c, j * P:(j + 1) * P] for a in w_v],
                              [a[:, c, :, 2 * j * SQ:2 * (j + 1) * SQ].rearrange("p b (h q) -> p h b q", h=2)
                               for a in fold], c == 0, False)
                    if j == 0:
                        pe.wait_ge(v_loaded.sem, v_loaded.at(t, 48))
                        pe.wait_ge(last_copy.sem, last_copy.at(t, GB))
                        pe.wait_ge(last_lo.sem, last_lo.at(t, GB))
                    pe.matmul(out, last_v[:, j * P:(j + 1) * P],
                              last_p[:, 2 * j:2 * j + 2, :, :].rearrange("p h b q -> p h (b q)"),
                              start=False, stop=True).then_inc(o_ready.sem, 1)

        @block.vector
        def _(dve):
            dve.sem_inc(o_lo_done.sem, 1)
            with dve.Fori(0, TURNS) as t:
                def row_max(b, i):
                    dve.wait_ge(scores_ready.sem, scores_ready.at(t, b * TILES + i + 1))
                    dve.tensor_reduce(negmax[:, i:i + 1], ps[:, S_BANK[i], 0:SK], AX_X, ALU.max, negate=True)\
                        .then_inc(max_done.sem, 1)

                def normalise(b, i):
                    dve.wait_ge(exp_done.sem, exp_done.at(t, b * TILES + i + 1))
                    dve.reciprocal(share[:, i:i + 1], total[:, i:i + 1]).then_inc(share_done.sem, 1)
                    dve.wait_ge(share_done.sem, share_done.at(t, b * TILES + i + 1))
                    dve.tensor_scalar(last_z[:, b, i, b:b + 1], prob[:, i, SK - 1:SK], share[:, i:i + 1], None,
                                      ALU.mult)
                    dve.tensor_scalar(prob[:, i, 0:KT * P], prob[:, i, 0:KT * P], share[:, i:i + 1], None,
                                      ALU.mult).then_inc(probs_ready.sem, 1)

                def split_probs(b):
                    for k in range(KT):
                        dve.wait_ge(pT_hi.sem, pT_hi.at(t, b * KT + k + 1))
                        dve.tensor_tensor(pT[1][:, k, :], ps[:, T_BANK[k], :], f32(pT[0][:, k, :]), ALU.subtract)\
                            .then_inc(pT_lo.sem, 1)
                    dve.wait_ge(last_hi.sem, last_hi.at(t, b + 1))
                    dve.wait_ge(last_copy.sem, last_copy.at(t, b + 1))
                    dve.tensor_tensor(last_p[64:64 + GB, :, b, :],
                                      ps[0:GB, L_BANK, :].rearrange("p (h q) -> p h q", q=SQ),
                                      f32(last_p[0:GB, :, b, :]), ALU.subtract).then_inc(last_lo.sem, 1)

                def split_mixed(b):
                    for c in range(DC):
                        dve.wait_ge(mixed_hi.sem, mixed_hi.at(t, b * DC + c + 1))
                        dve.tensor_tensor(fold[1][:, c, b, :], ps[:, M_BANK[c % 2], :], f32(fold[0][:, c, b, :]),
                                          ALU.subtract)\
                            .then_inc(mixed_lo.sem, 1)

                for j in range(PAIRS):
                    for u in range(2):
                        n = 2 * j + u
                        dve.wait_ge(fold_hi.sem, fold_hi.at(t, n + 1))
                        hi, lo = (pair_of_heads(a, j, u) for a in fold)
                        dve.tensor_tensor(lo, ps[:, FOLD_BANK[n % 4], :].rearrange("p (c n) -> p c n", n=2 * SQ),
                                          f32(hi), ALU.subtract).then_inc(fold_lo.sem, 1)
                    for i in SOFTMAX_AFTER.get(j, ()):
                        row_max(0, i)
                        if i > 0:
                            normalise(0, i - 1)
                normalise(0, TILES - 1)
                for b in range(1, GB + 1):
                    split_probs(b - 1)
                    if b < GB:
                        for i in range(TILES):
                            row_max(b, i)
                            if i > 0:
                                normalise(b, i - 1)
                        normalise(b, TILES - 1)
                    split_mixed(b - 1)
                for j in range(PAIRS):
                    dve.wait_ge(o_hi_done.sem, o_hi_done.at(t, 2 * j + 2))
                    for h in range(2):
                        r = slice(h * HE, (h + 1) * HE)
                        dve.tensor_tensor(o[j % 4][1][r, :], ps[r, O_BANK[j % 4], h * P:(h + 1) * P],
                                          f32(o[j % 4][0][r, :]), ALU.subtract).then_inc(o_lo_done.sem, 1)

        @block.scalar
        def _(act):
            for done in o_stored:
                act.sem_inc(done.sem, 32)
            with act.Fori(0, TURNS) as t:
                def split_T(b):
                    act.wait_ge(T_loaded.sem, T_loaded.at(t, 16 * (b + 1)))
                    act.wait_ge(scores_ready.sem, scores_ready.at(t, (b - 1) * TILES))
                    act.activation(cT[b % 2][0][:, :, 0:SK], raw_T[:, :, :], ACT.Copy).then_inc(Thi_done.sem, 1)

                def split_n(b):
                    act.wait_ge(n_loaded.sem, n_loaded.at(t, 16 * (b + 1)))
                    act.wait_ge(mixed.sem, mixed.at(t, (b - 1) * DC))
                    act.activation(cn[b % 2][0][:, :, :], raw_n[:, :, :], ACT.Copy).then_inc(nhi_done.sem, 1)

                def exps(b, i):
                    act.wait_ge(max_done.sem, max_done.at(t, b * TILES + i + 1))
                    act.activation(prob[:, i, 0:SK], ps[:, S_BANK[i], 0:SK], ACT.Exp,
                                   bias=negmax[:, i:i + 1], accum_out=total[:, i:i + 1]).then_inc(exp_done.sem, 1)

                def store_out(j):
                    act.wait_ge(o_lo_done.sem, o_lo_done.at(t, 2 * (j + 1)))
                    act.wait_ge(o_hi_done.sem, o_hi_done.at(t, 2 * (j + 1)))
                    for dst, src in zip((o_hi, o_lo), o[j % 4]):
                        act.dma_start(dst[j, :, bass.ds(t * P, P)], f32(src[:, :])).then_inc(o_stored[j % 4].sem, 16)

                for j in range(PAIRS):
                    if j == 1:
                        split_T(0)
                    for u in range(2):
                        n = 2 * j + u
                        act.wait_ge(fold_ready.sem, fold_ready.at(t, n + 1))
                        act.activation(pair_of_heads(fold[0], j, u),
                                       ps[:, FOLD_BANK[n % 4], :].rearrange("p (c n) -> p c n", n=2 * SQ), ACT.Copy)\
                            .then_inc(fold_hi.sem, 1)
                    for i in SOFTMAX_AFTER.get(j, ()):
                        exps(0, i)
                    if j == 4:
                        split_n(0)
                    if j == 6:
                        split_T(1)
                for b in range(1, GB + 1):
                    for k in range(KT):
                        act.wait_ge(turned.sem, turned.at(t, (b - 1) * KT + k + 1))
                        act.activation(pT[0][:, k, :], ps[:, T_BANK[k], :], ACT.Copy).then_inc(pT_hi.sem, 1)
                    act.wait_ge(last_turned.sem, last_turned.at(t, b))
                    row = ps[0:GB, L_BANK, :].rearrange("p (h q) -> p h q", q=SQ)
                    act.activation(last_p[0:GB, :, b - 1, :], row, ACT.Copy).then_inc(last_hi.sem, 1)
                    act.activation(last_p[32:32 + GB, :, b - 1, :], row, ACT.Copy).then_inc(last_copy.sem, 1)
                    if b == 1:
                        split_n(1)
                    if b < GB - 1:
                        split_T(b + 1)
                    if b < GB:
                        for i in range(TILES):
                            exps(b, i)
                    for c in range(DC):
                        act.wait_ge(mixed.sem, mixed.at(t, (b - 1) * DC + c + 1))
                        act.activation(fold[0][:, c, b - 1, :], ps[:, M_BANK[c % 2], :], ACT.Copy)\
                            .then_inc(mixed_hi.sem, 1)
                    if b + 1 < GB:
                        split_n(b + 1)
                for j in range(PAIRS):
                    act.wait_ge(o_ready.sem, o_ready.at(t, j + 1))
                    act.wait_ge(o_stored[j % 4].sem, o_stored[j % 4].at(t, 32 * (j // 4)))
                    for h in range(2):
                        r = slice(h * HE, (h + 1) * HE)
                        act.activation(o[j % 4][0][r, :], ps[r, O_BANK[j % 4], h * P:(h + 1) * P], ACT.Copy)\
                            .then_inc(o_hi_done.sem, 1)
                    if j > 0:
                        store_out(j - 1)
                store_out(PAIRS - 1)
            for done in o_stored:
                act.wait_ge(done.sem, 32 + TURNS * done.per)


def last_values(nc, last_T, w_v, v_hi, v_lo):
    dim, B = last_T.shape
    DC, inner = w_v[0].shape[1], w_v[0].shape[2]
    with ExitStack() as ctx:
        s = Scope(nc, ctx, "v")
        lT = s.pair("lT", [P, DC, B])
        raw = s.sb("raw", [P, DC, B])
        v = s.pair("v", [B, inner])
        ps = s.psum()
        loaded, hi_done, lo_done, ready = s.sem("loaded"), s.sem("hi_done"), s.sem("lo_done"), s.sem("ready")
        vhi_done, vlo_done, stored = s.sem("vhi_done"), s.sem("vlo_done"), s.sem("stored")
        block = ctx.enter_context(nc.Block())
        acc = ps[0:B, 0:2, :]

        @block.sync
        def _(sp):
            sp.dma_start(raw[:, :, :], last_T.rearrange("(c p) b -> p c b", p=P)).then_inc(loaded, 16)
            sp.wait_ge(vhi_done, 1)
            sp.dma_start(v_hi, f32(v[0][:, :])).then_inc(stored, 16)
            sp.wait_ge(vlo_done, 1)
            sp.dma_start(v_lo, f32(v[1][:, :])).then_inc(stored, 16)
            sp.wait_ge(stored, 32)

        @block.scalar
        def _(act):
            act.wait_ge(loaded, 16)
            act.activation(lT[0][:, :, :], raw[:, :, :], ACT.Copy).then_inc(hi_done, 1)
            act.wait_ge(ready, 2)
            act.activation(v[0][:, :].rearrange("p (h n) -> p h n", h=2), acc, ACT.Copy).then_inc(vhi_done, 1)

        @block.vector
        def _(dve):
            dve.wait_ge(hi_done, 1)
            dve.tensor_tensor(lT[1][:, :, :], raw[:, :, :], f32(lT[0][:, :, :]), ALU.subtract).then_inc(lo_done, 1)
            dve.wait_ge(vhi_done, 1)
            dve.tensor_tensor(v[1][:, :].rearrange("p (h n) -> p h n", h=2), acc,
                              f32(v[0][:, :]).rearrange("p (h n) -> p h n", h=2), ALU.subtract).then_inc(vlo_done, 1)

        @block.tensor
        def _(pe):
            pe.wait_ge(lo_done, 1)
            for h in range(2):
                for c in range(DC):
                    mm = three(pe, ps[0:B, h, :], [a[:, c, :] for a in lT],
                               [a[:, c, h * 512:(h + 1) * 512] for a in w_v], c == 0, c == DC - 1)
                mm.then_inc(ready, 1)


def head_attention(nc, x, out_w, bias, gate, wqkv, o_hi, o_lo, qkv, mixed_dram, x2, identity, block_mask):
    tokens, dim = x.shape
    PAIRS, DC, TT = out_w.shape[0] // P, dim // P, 4
    TURNS = tokens // (TT * P)
    H, HD = 16, dim // 16
    GT = P // H
    GROUPS = P // GT
    with ExitStack() as ctx:
        s = Scope(nc, ctx, "a")
        wo = s.pair("wo", [P, PAIRS * dim])
        w3 = [s.pair(f"w{k}", [P, DC * dim]) for k in range(3)]
        pieces = []
        for src, dst in [(out_w, wo)] + list(zip(wqkv, w3)):
            v = src.rearrange("(c p) n -> c p n", p=P)
            pieces += [(v[c], dst[0][:, c * dim:(c + 1) * dim], dst[1][:, c * dim:(c + 1) * dim])
                       for c in range(v.shape[0])]
        w_split, ALL = WeightSplit(s, pieces, dim), range(len(pieces))
        wo = [a[:, :].rearrange("p (j n) -> p j n", j=PAIRS) for a in wo]
        w3 = [[a[:, :].rearrange("p (c n) -> p c n", c=DC) for a in w] for w in w3]

        oT = [s.pair(f"oT{i}", [P, PAIRS, P]) for i in range(2)]
        xin = [s.sb(f"xin{i}", [P, dim]) for i in range(2)]
        x1 = [s.sb(f"x1{i}", [P, dim]) for i in range(4)]
        y, xn, xo, x2o = s.sb("y", [P, dim]), s.sb("xn", [P, 1, dim]), s.sb("xo", [P, dim]), s.sb("x2o", [P, dim])
        xT = s.pair("xT", [P, DC * P])
        qs, ks, vs = s.sb("qs", [P, dim]), s.sb("ks", [P, dim]), s.sb("vs", [P, dim])
        qmax, kmax = s.sb("qmax", [P, H]), s.sb("kmax", [P, HD])
        sums, inv = s.sb("sums", [P, H + HD]), s.sb("inv", [P, H + HD])
        q_rows, k_rows, v_rows = (s.sb(n, [P, GROUPS, HD]) for n in ("q_rows", "k_rows", "v_rows"))
        qT, kT = s.sb("qT", [P, 4, P]), s.sb("kT", [P, 4, P])
        weights = s.sb("weights", [P, 4, 4 * P])
        od = s.sb("od", [P, GROUPS, HD])
        bias_b, gate_b, tanh_b = s.sb("bias", [P, dim]), s.sb("gate", [P, 1]), s.sb("tanh", [P, 1])
        mask, ident = s.sb("mask", [P, P]), s.sb("ident", [P, P])
        stats, moments = s.sb("stats", [P, 1, 6]), s.sb("moments", [P, 1, 2])
        shifted, rstd, power = s.sb("shifted", [P, 1]), s.sb("rstd", [P, 1]), s.sb("power", [P, 1])
        ps = s.psum()
        Y, V, OUT, Q, K, W, XT = 0, 0, 1, 2, 3, 4, 4

        once, power_set, tanh_done = s.sem("once"), s.sem("power_set"), s.sem("tanh_done")
        in_loaded = [s.count(f"in_loaded{i}", 48 * TT // 2) for i in range(2)]
        NORM_STEPS, SOFTMAX_STEPS = 2, 4
        DVE_STEPS = (NORM_STEPS + SOFTMAX_STEPS) * TT
        DVE_BEFORE = 3 * NORM_STEPS + 2 * SOFTMAX_STEPS
        chain_sem = s.sem("dve_chain")
        y_ready, y_free = s.count("y_ready", TT, 1), s.count("y_free", TT)
        x1_done = s.count("x1_done", TT, 1)
        var_ready, rstd_done = s.count("var_ready", TT), s.count("rstd_done", TT)
        normed = s.count("normed", TT)
        x_turned, xhi_done, xlo_done = s.count("x_turned", TT), s.count("xhi_done", TT), s.count("xlo_done", TT)
        q_ready, k_ready, v_ready = s.count("q_ready", TT), s.count("k_ready", TT), s.count("v_ready", TT)
        q_shift, k_shift = s.count("q_shift", TT), s.count("k_shift", TT)
        q_exp, k_exp = s.count("q_exp", TT), s.count("k_exp", TT)
        q_done, k_done = s.count("q_done", TT), s.count("k_done", TT)
        v_done = s.count("v_done", TT, 1)
        v_written, kq_written = s.count("v_written", 16 * TT, 16), s.count("kq_written", 32 * TT, 32)
        v_read, kq_read = s.count("v_read", 16 * TT), s.count("kq_read", 32 * TT)
        q_turned, k_turned = s.count("q_turned", TT, 1), s.count("k_turned", TT)
        qT_done, kT_done = s.count("qT_done", TT, 1), s.count("kT_done", TT, 1)
        dots_ready, masked = s.count("dots_ready", 4 * TT), s.count("masked", 4 * TT)
        out_ready, out_done = s.count("out_ready", TT, 1), s.count("out_done", TT, 1)
        out_written, out_read = s.count("out_written", 16 * TT, 16), s.count("out_read", 16 * TT)
        x2_done, x2_stored = s.count("x2_done", TT, 1), s.count("x2_stored", 16 * TT, 16)
        block = ctx.enter_context(nc.Block())

        def there(t, i):
            return not isinstance(t, int) or 0 <= t * TT + i < TURNS * TT

        def all_steps(eng, step):
            for i in (-1, 0, 1):
                step(0, i)
            with eng.Fori(0, TURNS - 1) as t:
                for i in range(2, 2 + TT):
                    step(t, i)
            for i in range(2, 2 + TT):
                step(TURNS - 1, i)

        @block.gpsimd
        def _(pool):
            def load(t, i):
                n = t * (TT * P) + i * P
                for dst, src in zip(oT[i % 2], (o_hi, o_lo)):
                    pool.dma_start(f32(dst[:, :, :]), src[:, :, bass.ds(n, P)].rearrange("j p n -> p j n"))\
                        .then_inc(in_loaded[i % 2].sem, 16)
                pool.dma_start(xin[i % 2][:, :], x[bass.ds(n, P), :]).then_inc(in_loaded[i % 2].sem, 16)

            def step(t, i):
                if there(t, i + 2):
                    pool.wait_ge(y_ready.sem, y_ready.at(t, i + 1))
                    pool.wait_ge(x1_done.sem, x1_done.at(t, i + 1))
                    load(t, i + 2)
                if there(t, i + 1):
                    pool.wait_ge(var_ready.sem, var_ready.at(t, i + 2))
                    pool.tensor_tensor(rstd[:, :], shifted[:, :], power[:, :], ALU.pow).then_inc(rstd_done.sem, 1)

            pool.memset(power[:, :], -0.5).then_inc(power_set, 1)
            pool.wait_ge(power_set, 1)
            load(0, 0)
            pool.wait_ge(w_split.lo_done, PAIRS)
            all_steps(pool, step)

        @block.sync
        def _(sp):
            for dst, src in ((ident[:, :], identity), (mask[:, :], block_mask),
                             (bias_b[:, :], bias.partition_broadcast(P)), (gate_b[:, :], gate.partition_broadcast(P))):
                sp.dma_start(dst, src).then_inc(once, 16)
            w_split.load(sp, ALL)

            def tile(ap, t, i):
                return ap[bass.ds(t * (TT * P) + i * P, P), :]

            def turned_rows(ap, t, i):
                return tile(ap, t, i).rearrange("(g t) (h e) -> (t h) g e", t=GT, h=H)

            def step(t, i):
                if there(t, i):
                    sp.wait_ge(v_done.sem, v_done.at(t, i + 1))
                    sp.dma_start(tile(qkv[2], t, i), vs[:, :]).then_inc(v_written.sem, 16)
                    sp.wait_ge(k_done.sem, k_done.at(t, i + 1))
                    sp.wait_ge(q_done.sem, q_done.at(t, i + 1))
                    sp.dma_start(tile(qkv[1], t, i), ks[:, :]).then_inc(kq_written.sem, 16)
                    sp.dma_start(tile(qkv[0], t, i), qs[:, :]).then_inc(kq_written.sem, 16)
                    sp.wait_ge(kq_written.sem, kq_written.at(t, 32 * (i + 1)))
                    sp.wait_ge(q_turned.sem, q_turned.at(t, i))
                    sp.dma_start(k_rows[:, :, :], turned_rows(qkv[1], t, i)).then_inc(kq_read.sem, 16)
                    sp.dma_start(q_rows[:, :, :], turned_rows(qkv[0], t, i)).then_inc(kq_read.sem, 16)
                if there(t, i - 2):
                    sp.wait_ge(x2_done.sem, x2_done.at(t, i - 1))
                    sp.dma_start(tile(x2, t, i - 2), x2o[:, :]).then_inc(x2_stored.sem, 16)
                if there(t, i):
                    sp.wait_ge(v_written.sem, v_written.at(t, 16 * (i + 1)))
                    sp.wait_ge(out_ready.sem, out_ready.at(t, i))
                    sp.dma_start(v_rows[:, :, :], turned_rows(qkv[2], t, i)).then_inc(v_read.sem, 16)
                if there(t, i - 1):
                    sp.wait_ge(out_done.sem, out_done.at(t, i))
                    sp.dma_start(turned_rows(mixed_dram, t, i - 1), od[:, :, :]).then_inc(out_written.sem, 16)
                    sp.wait_ge(out_written.sem, out_written.at(t, 16 * i))
                    sp.wait_ge(x2_done.sem, x2_done.at(t, i - 1))
                    sp.dma_start(xo[:, :], tile(mixed_dram, t, i - 1)).then_inc(out_read.sem, 16)

            all_steps(sp, step)
            sp.wait_ge(x2_stored.sem, 16 + TURNS * x2_stored.per)

        @block.tensor
        def _(pe):
            def step(t, i):
                if there(t, i):
                    pe.wait_ge(normed.sem, normed.at(t, i + 1))
                    for c in range(DC):
                        mm = pe.transpose(ps[:, XT, c * P:(c + 1) * P], xn[:, 0, c * P:(c + 1) * P], ident[:, :])
                    mm.then_inc(x_turned.sem, 1)
                if there(t, i - 1):
                    pe.wait_ge(kq_read.sem, kq_read.at(t, 32 * i))
                    for rows, bank, done in ((k_rows, K, k_turned), (q_rows, Q, q_turned)):
                        for u in range(4):
                            mm = pe.transpose(ps[:, bank, u * P:(u + 1) * P],
                                              rows[:, 4 * u:4 * u + 4, :].rearrange("p g e -> p (g e)"), ident[:, :])
                        mm.then_inc(done.sem, 1)
                if there(t, i):
                    pe.wait_ge(w_split.lo_done, len(pieces))
                    pe.wait_ge(xlo_done.sem, xlo_done.at(t, i + 1))
                    for k, bank, done, free, n in ((2, V, v_ready, y_free, i + 1), (1, K, k_ready, kT_done, i),
                                                   (0, Q, q_ready, qT_done, i)):
                        pe.wait_ge(free.sem, free.at(t, n))
                        for c in range(DC):
                            mm = three(pe, ps[:, bank, :], [a[:, c * P:(c + 1) * P] for a in xT],
                                       [a[:, c, :] for a in w3[k]], c == 0, c == DC - 1)
                        mm.then_inc(done.sem, 1)
                if there(t, i + 1):
                    pe.wait_ge(in_loaded[(i + 1) % 2].sem,
                               in_loaded[(i + 1) % 2].at(t, 48 * ((i + 1) // 2 + 1)))
                    pe.wait_ge(v_done.sem, v_done.at(t, i + 1))
                    for j in range(PAIRS):
                        mm = three(pe, ps[:, Y, :], [a[:, j, :] for a in oT[(i + 1) % 2]],
                                   [a[:, j, :] for a in wo], j == 0, j == PAIRS - 1)
                    mm.then_inc(y_ready.sem, 1)
                if there(t, i - 1):
                    pe.wait_ge(qT_done.sem, qT_done.at(t, i))
                    pe.wait_ge(kT_done.sem, kT_done.at(t, i))
                    for r in range(4):
                        g = slice(r * HD, (r + 1) * HD)
                        for u in range(4):
                            mm = pe.matmul(ps[:, W + r, u * P:(u + 1) * P], kT[g, u, :], qT[g, u, :],
                                           start=True, stop=True)
                        mm.then_inc(dots_ready.sem, 1)
                    pe.wait_ge(v_read.sem, v_read.at(t, 16 * i))
                    pe.wait_ge(out_done.sem, out_done.at(t, i - 1))
                    for r in range(4):
                        pe.wait_ge(masked.sem, masked.at(t, 4 * (i - 1) + r + 1))
                        for u in range(4):
                            g = 4 * u + r
                            mm = pe.matmul(ps[:, OUT, g * HD:(g + 1) * HD], weights[:, r, u * P:(u + 1) * P],
                                           v_rows[:, g, :], start=True, stop=True)
                    mm.then_inc(out_ready.sem, 1)

            for done in (y_ready, q_turned, out_ready):
                pe.sem_inc(done.sem, 1)
            pe.wait_ge(once, 64)
            pe.wait_ge(w_split.lo_done, PAIRS)
            all_steps(pe, step)

        @block.scalar
        def _(act):
            def step(t, i):
                if there(t, i):
                    act.wait_ge(x_turned.sem, x_turned.at(t, i + 1))
                    act.activation(xT[0][:, :], ps[:, XT, :], ACT.Copy).then_inc(xhi_done.sem, 1)
                if there(t, i - 1):
                    act.wait_ge(q_turned.sem, q_turned.at(t, i))
                    act.activation(qT[:, :, :], ps[:, Q, :].rearrange("p (u n) -> p u n", u=4), ACT.Copy)\
                        .then_inc(qT_done.sem, 1)
                if there(t, i):
                    act.wait_ge(v_ready.sem, v_ready.at(t, i + 1))
                    act.wait_ge(v_written.sem, v_written.at(t, 16 * i))
                    act.activation(vs[:, :], ps[:, V, :], ACT.Copy).then_inc(v_done.sem, 1)
                    for src, shift, done in ((ks, k_shift, k_exp), (qs, q_shift, q_exp)):
                        act.wait_ge(shift.sem, shift.at(t, i + 1))
                        act.activation(src[:, :], src[:, :], ACT.Exp).then_inc(done.sem, 1)
                if there(t, i - 1):
                    act.wait_ge(out_ready.sem, out_ready.at(t, i))
                    act.wait_ge(out_written.sem, out_written.at(t, 16 * (i - 1)))
                    act.activation(od[:, :, :], ps[:, OUT, :].rearrange("p (g e) -> p g e", g=GROUPS), ACT.Copy)\
                        .then_inc(out_done.sem, 1)

            act.sem_inc(v_done.sem, 1)
            act.sem_inc(qT_done.sem, 1)
            act.sem_inc(out_done.sem, 1)
            act.sem_inc(v_written.sem, 16)
            act.sem_inc(kq_written.sem, 32)
            act.sem_inc(out_written.sem, 16)
            act.sem_inc(x2_stored.sem, 16)
            act.wait_ge(once, 64)
            act.activation(tanh_b[:, :], gate_b[:, :], ACT.Tanh).then_inc(tanh_done, 1)
            w_split.round(act, ALL)
            all_steps(act, step)

        @block.vector
        def _(dve):
            def by_head(ap):
                return ap.rearrange("p (h e) -> p h e", h=H)

            def heads_last(ap):
                return ap.rearrange("p (h e) -> p e h", h=H)

            def each_head(ap):
                return ap.rearrange("p (h e) -> p h e", e=1).to_broadcast([P, H, HD])

            def each_element(ap):
                return ap.rearrange("p (h e) -> p h e", h=1).to_broadcast([P, H, HD])

            def softmaxes(t, i, chain):
                dve.wait_ge(kq_written.sem, kq_written.at(t, 32 * i))
                dve.wait_ge(k_ready.sem, k_ready.at(t, i + 1))
                chain.step(dve.tensor_reduce(kmax[:, :], heads_last(ps[:, K, :]), AX_X, ALU.max))
                dve.tensor_tensor(by_head(ks[:, :]), by_head(ps[:, K, :]), each_element(kmax[:, :]), ALU.subtract)\
                    .then_inc(k_shift.sem, 1)
                dve.wait_ge(q_ready.sem, q_ready.at(t, i + 1))
                chain.step(dve.tensor_reduce(qmax[:, :], by_head(ps[:, Q, :]), AX_X, ALU.max))
                dve.tensor_tensor(by_head(qs[:, :]), by_head(ps[:, Q, :]), each_head(qmax[:, :]), ALU.subtract)\
                    .then_inc(q_shift.sem, 1)
                dve.wait_ge(k_exp.sem, k_exp.at(t, i + 1))
                dve.tensor_reduce(sums[:, H:], heads_last(ks[:, :]), AX_X, ALU.add)
                dve.wait_ge(q_exp.sem, q_exp.at(t, i + 1))
                chain.step(dve.tensor_reduce(sums[:, 0:H], by_head(qs[:, :]), AX_X, ALU.add))
                chain.step(dve.reciprocal(inv[:, :], sums[:, :]))
                dve.tensor_tensor(by_head(ks[:, :]), by_head(ks[:, :]), each_element(inv[:, H:]), ALU.mult)\
                    .then_inc(k_done.sem, 1)
                dve.tensor_tensor(by_head(qs[:, :]), by_head(qs[:, :]), each_head(inv[:, 0:H]), ALU.mult)\
                    .then_inc(q_done.sem, 1)

            def step(t, i, chain):
                if there(t, i):
                    dve.wait_ge(xhi_done.sem, xhi_done.at(t, i + 1))
                    dve.tensor_tensor(xT[1][:, :], ps[:, XT, :], f32(xT[0][:, :]), ALU.subtract)\
                        .then_inc(xlo_done.sem, 1)
                if there(t, i - 1):
                    dve.wait_ge(k_turned.sem, k_turned.at(t, i))
                    dve.tensor_copy(kT[:, :, :], ps[:, K, :].rearrange("p (u n) -> p u n", u=4))\
                        .then_inc(kT_done.sem, 1)
                if there(t, i):
                    softmaxes(t, i, chain)
                if there(t, i - 2):
                    dve.wait_ge(out_read.sem, out_read.at(t, 16 * (i - 1)))
                    dve.wait_ge(x2_stored.sem, x2_stored.at(t, 16 * (i - 2)))
                    dve.tensor_tensor(x2o[:, :], x1[(i - 2) % 4][:, :], xo[:, :], ALU.add).then_inc(x2_done.sem, 1)
                if there(t, i + 1):
                    n = i + 1
                    dve.wait_ge(y_ready.sem, y_ready.at(t, n + 1))
                    dve.tensor_tensor(y[:, :], ps[:, Y, :], bias_b[:, :], ALU.add).then_inc(y_free.sem, 1)
                    dve.wait_ge(y_free.sem, y_free.at(t, n + 1))
                    dve.wait_ge(in_loaded[n % 2].sem, in_loaded[n % 2].at(t, 48 * (n // 2 + 1)))
                    dve.scalar_tensor_tensor(x1[n % 4][:, :], y[:, :], tanh_b[:, 0:1], xin[n % 2][:, :], ALU.mult,
                                             ALU.add).then_inc(x1_done.sem, 1)
                    dve.wait_ge(x1_done.sem, x1_done.at(t, n + 1))
                    src = x1[n % 4][:, :].rearrange("p (i d) -> p i d", i=1)
                    norm_moments(dve, chain, src, stats, moments, shifted, 1, var_ready)
                for r in range(4):
                    if there(t, i - 1):
                        dve.wait_ge(dots_ready.sem, dots_ready.at(t, 4 * (i - 1) + r + 1))
                        dve.tensor_tensor(weights[:, r, :].rearrange("p (u n) -> p u n", u=4),
                                          ps[:, W + r, :].rearrange("p (u n) -> p u n", u=4),
                                          mask[:, :].rearrange("p (u n) -> p u n", u=1).to_broadcast([P, 4, P]),
                                          ALU.mult).then_inc(masked.sem, 1)
                    if r == 1 and there(t, i + 1):
                        dve.wait_ge(rstd_done.sem, rstd_done.at(t, n + 1))
                        norm_scale(dve, xn, src, moments, rstd, 1).then_inc(normed.sem, 1)

            dve.sem_inc(x1_done.sem, 1)
            dve.sem_inc(kT_done.sem, 1)
            dve.sem_inc(x2_done.sem, 1)
            dve.wait_ge(once, 64)
            dve.wait_ge(tanh_done, 1)
            w_split.split(dve, ALL)
            chain = Chain(dve, chain_sem, 0, DVE_STEPS)
            for i in (-1, 0, 1):
                step(0, i, chain)
            assert chain.n == DVE_BEFORE
            with dve.Fori(0, TURNS - 1) as t:
                chain = Chain(dve, chain_sem, t, DVE_STEPS, DVE_BEFORE)
                for i in range(2, 2 + TT):
                    step(t, i, chain)
                assert chain.n == DVE_BEFORE + DVE_STEPS
            chain = Chain(dve, chain_sem, TURNS - 1, DVE_STEPS, DVE_BEFORE)
            for i in range(2, 2 + TT):
                step(TURNS - 1, i, chain)


def gated_mlp(nc, x2, wg, wu, wd, out, identity, scale):
    tokens, dim = x2.shape
    hidden = wg.shape[1]
    DC, HC, TT = dim // P, hidden // P, 4
    N = TT * P
    TURNS = tokens // N
    with ExitStack() as ctx:
        s = Scope(nc, ctx, "f")
        w_g, w_u, w_d = s.pair("wg", [P, DC * hidden]), s.pair("wu", [P, DC * hidden]), s.pair("wd", [P, HC * dim])
        pieces = []
        width = dim
        for src, dst in ((wg, w_g), (wu, w_u), (wd, w_d)):
            v = src.rearrange("(c p) n -> c p n", p=P)
            n = v.shape[2]
            for c in range(v.shape[0]):
                for a in range(0, n, width):
                    b = c * n + a
                    pieces.append((v[c, :, a:a + width], dst[0][:, b:b + width], dst[1][:, b:b + width]))
        w_split = WeightSplit(s, pieces, width, mybir.dt.int32, scale)
        FIRST, ALL = w_split.RING, len(pieces)
        GATE_UP = ALL - HC
        w_g, w_u = ([a[:, :].rearrange("p (c n) -> p c n", c=DC) for a in w] for w in (w_g, w_u))
        w_d = [a[:, :].rearrange("p (c n) -> p c n", c=HC) for a in w_d]

        xn, y = s.sb("xn", [P, TT, dim]), s.sb("y", [P, TT, dim])
        xT = s.pair("xT", [P, DC, N])
        sig, gated, h32 = s.sb("sig", [P, N]), s.sb("gated", [P, N]), s.sb("h32", [P, N])
        h = [s.pair(f"h{i}", [P, N]) for i in range(2)]
        stats, moments = s.sb("stats", [P, TT, 6]), s.sb("moments", [P, TT, 2])
        shifted, rstd, power = s.sb("shifted", [P, TT]), s.sb("rstd", [P, TT]), s.sb("power", [P, TT])
        ident = s.sb("ident", [P, P])
        ps = s.psum()
        once, power_set = s.sem("once"), s.sem("power_set")
        x_loaded, y_loaded = s.count("x_loaded", 16), s.count("y_loaded", 16)
        stored = s.count("stored", 16 * TT, 16)
        chain_sem = s.sem("dve_chain")
        DVE_STEPS = 2
        var_ready, rstd_done, normed = s.count("var_ready", 1), s.count("rstd_done", 1), s.count("normed", 1)
        turned, xhi_done, xlo_done = s.count("turned", DC), s.count("xhi_done", DC), s.count("xlo_done", DC)
        gate_ready, up_ready = s.count("gate_ready", HC), s.count("up_ready", HC)
        sig_done, gated_done = s.count("sig_done", HC), s.count("gated_done", HC)
        h_done, hhi_done, hlo_done = s.count("h_done", HC), s.count("hhi_done", HC), s.count("hlo_done", HC)
        down_done = s.count("down_done", HC - 1)
        y_ready, y_done = s.count("y_ready", TT), s.count("y_done", TT, 1)
        block = ctx.enter_context(nc.Block())
        XT, G, U = 4, 4, 5

        @block.sync
        def _(sp):
            def load(dst, of_turn, done):
                sp.dma_start(dst[:, :, :], x2[bass.ds(of_turn * N, N), :].rearrange("(i p) d -> p i d", p=P))\
                    .then_inc(done.sem, 16)

            def turn(t, more):
                sp.wait_ge(stored.sem, stored.at(t, 0))
                load(y, t, y_loaded)
                if more:
                    sp.wait_ge(turned.sem, turned.at(t, DC))
                    load(xn, t + 1, x_loaded)
                for i in range(TT):
                    sp.wait_ge(y_done.sem, y_done.at(t, i + 1))
                    sp.dma_start(out[bass.ds(t * N + i * P, P), :], y[:, i, :]).then_inc(stored.sem, 16)

            sp.dma_start(ident[:, :], identity).then_inc(once, 16)
            w_split.load(sp, range(FIRST))
            load(xn, 0, x_loaded)
            w_split.load(sp, range(FIRST, ALL))
            with sp.Fori(0, TURNS - 1) as t:
                turn(t, True)
            turn(TURNS - 1, False)
            sp.wait_ge(stored.sem, 16 + TURNS * stored.per)

        @block.gpsimd
        def _(pool):
            pool.memset(power[:, :], -0.5).then_inc(power_set, 1)
            pool.wait_ge(power_set, 1)
            with pool.Fori(0, TURNS) as t:
                pool.wait_ge(var_ready.sem, var_ready.at(t, 1))
                pool.tensor_tensor(rstd[:, :], shifted[:, :], power[:, :], ALU.pow).then_inc(rstd_done.sem, 1)

        @block.vector
        def _(dve):
            def moments_of(t, ahead, chain):
                dve.wait_ge(x_loaded.sem, x_loaded.at(t, 16 * (ahead + 1)))
                norm_moments(dve, chain, xn, stats, moments, shifted, TT, var_ready)

            def norm(t, ahead):
                dve.wait_ge(rstd_done.sem, rstd_done.at(t, ahead + 1))
                norm_scale(dve, xn, xn, moments, rstd, TT).then_inc(normed.sem, 1)

            def split_x(t, ahead):
                for c in range(DC):
                    dve.wait_ge(xhi_done.sem, xhi_done.at(t, DC * ahead + c + 1))
                    dve.tensor_tensor(xT[1][:, c, :], ps[:, XT + c, :], f32(xT[0][:, c, :]), ALU.subtract)\
                        .then_inc(xlo_done.sem, 1)

            def turn(t, more, chain):
                for k in range(HC):
                    if k == 5 and more:
                        moments_of(t, 1, chain)
                    if k == 7 and more:
                        norm(t, 1)
                    dve.wait_ge(sig_done.sem, sig_done.at(t, k + 1))
                    dve.tensor_tensor(gated[:, :], ps[:, G + 2 * (k % 2), :], sig[:, :], ALU.mult)\
                        .then_inc(gated_done.sem, 1)
                    dve.wait_ge(gated_done.sem, gated_done.at(t, k + 1))
                    dve.wait_ge(up_ready.sem, up_ready.at(t, k + 1))
                    dve.tensor_tensor(h32[:, :], ps[:, U + 2 * (k % 2), :], gated[:, :], ALU.mult)\
                        .then_inc(h_done.sem, 1)
                    dve.wait_ge(hhi_done.sem, hhi_done.at(t, k + 1))
                    dve.tensor_tensor(h[k % 2][1][:, :], h32[:, :], f32(h[k % 2][0][:, :]), ALU.subtract)\
                        .then_inc(hlo_done.sem, 1)
                if more:
                    split_x(t, 1)
                dve.wait_ge(y_loaded.sem, y_loaded.at(t, 16))
                for i in range(TT):
                    dve.wait_ge(y_ready.sem, y_ready.at(t, i + 1))
                    dve.tensor_tensor(y[:, i, :], ps[:, i, :], y[:, i, :], ALU.add).then_inc(y_done.sem, 1)

            dve.sem_inc(y_done.sem, 1)
            w_split.split(dve, range(FIRST))
            moments_of(0, 0, Chain(dve, chain_sem, 0, DVE_STEPS))
            norm(0, 0)
            w_split.split(dve, range(FIRST, GATE_UP))
            split_x(0, 0)
            w_split.split(dve, range(GATE_UP, ALL))
            with dve.Fori(0, TURNS - 1) as t:
                turn(t, True, Chain(dve, chain_sem, t, DVE_STEPS, DVE_STEPS))
            turn(TURNS - 1, False, None)

        @block.scalar
        def _(act):
            def round_x(t, ahead):
                for c in range(DC):
                    act.wait_ge(turned.sem, turned.at(t, DC * ahead + c + 1))
                    act.activation(xT[0][:, c, :], ps[:, XT + c, :], ACT.Copy).then_inc(xhi_done.sem, 1)

            def turn(t, more):
                for k in range(HC):
                    act.wait_ge(gate_ready.sem, gate_ready.at(t, k + 1))
                    if k > 0:
                        act.wait_ge(gated_done.sem, gated_done.at(t, k))
                    act.activation(sig[:, :], ps[:, G + 2 * (k % 2), :], ACT.Sigmoid).then_inc(sig_done.sem, 1)
                    act.wait_ge(h_done.sem, h_done.at(t, k + 1))
                    if k >= 2:
                        act.wait_ge(down_done.sem, down_done.at(t, k - 1))
                    act.activation(h[k % 2][0][:, :], h32[:, :], ACT.Copy).then_inc(hhi_done.sem, 1)
                if more:
                    round_x(t, 1)

            act.sem_inc(stored.sem, 16)
            w_split.round(act, range(GATE_UP))
            round_x(0, 0)
            w_split.round(act, range(GATE_UP, ALL))
            with act.Fori(0, TURNS - 1) as t:
                turn(t, True)
            turn(TURNS - 1, False)

        @block.tensor
        def _(pe):
            def turn_x(t, ahead, chunks):
                pe.wait_ge(normed.sem, normed.at(t, ahead + 1))
                for c in chunks:
                    for i in range(TT):
                        mm = pe.transpose(ps[:, XT + c, i * P:(i + 1) * P], xn[:, i, c * P:(c + 1) * P], ident[:, :])
                    mm.then_inc(turned.sem, 1)

            def gate_up(t, k):
                if k >= 2:
                    pe.wait_ge(h_done.sem, h_done.at(t, k - 1))
                for w, bank, done in ((w_g, G, gate_ready), (w_u, U, up_ready)):
                    for c in range(DC):
                        if k == 0 and bank == G:
                            pe.wait_ge(xlo_done.sem, xlo_done.at(t, c + 1))
                        mm = three(pe, ps[:, bank + 2 * (k % 2), :], [a[:, c, k * P:(k + 1) * P] for a in w],
                                   [a[:, c, :] for a in xT], c == 0, c == DC - 1)
                    mm.then_inc(done.sem, 1)

            def down(t, k):
                pe.wait_ge(hlo_done.sem, hlo_done.at(t, k + 1))
                if k == 0:
                    pe.wait_ge(w_split.lo_done, ALL)
                    pe.wait_ge(y_done.sem, y_done.at(t, 0))
                for i in range(TT):
                    mm = three(pe, ps[:, i, :], [a[:, i * P:(i + 1) * P] for a in h[k % 2]],
                               [a[:, k, :] for a in w_d], k == 0, k == HC - 1)
                    if k == HC - 1:
                        mm.then_inc(y_ready.sem, 1)
                if k < HC - 1:
                    mm.then_inc(down_done.sem, 1)

            def turn(t, more):
                gate_up(t, 0)
                for k in range(1, HC):
                    gate_up(t, k)
                    down(t, k - 1)
                if more:
                    pe.wait_ge(h_done.sem, h_done.at(t, HC - 1))
                    turn_x(t, 1, (0, 1))
                down(t, HC - 1)
                if more:
                    pe.wait_ge(h_done.sem, h_done.at(t, HC))
                    turn_x(t, 1, (2, 3))

            pe.wait_ge(once, 16)
            turn_x(0, 0, range(DC))
            pe.wait_ge(w_split.lo_done, GATE_UP)
            with pe.Fori(0, TURNS - 1) as t:
                turn(t, True)
            turn(TURNS - 1, False)


def build(nc, x, ctx_nat, ctx_T, last_T, gamma, beta, wq, wkT, wv, w_out, b_out, gate, aq, ak, av, wg, wu, wd,
          identity, block_mask, out):
    tokens, dim = x.shape
    inner = wq.shape[1]
    B = ctx_nat.shape[0]

    def scratch(name, shape, dt=F32):
        return nc.dram_tensor(name, shape, dt, kind="Internal").ap()

    q_dram = scratch("q", [P, inner // P, 2, tokens])
    o_hi, o_lo = (scratch(n, [inner // P, P, tokens]) for n in ("o_hi", "o_lo"))
    v_hi, v_lo = (scratch(n, [B, inner]) for n in ("v_hi", "v_lo"))
    qkv, mixed, x2 = scratch("qkv", [3, tokens, dim]), scratch("mixed", [tokens, dim]), scratch("x2", [tokens, dim])
    HEADS = 16
    project_queries(nc, x, gamma, beta, wq, q_dram, identity, (inner // HEADS) ** -0.5)
    cross_attention(nc, ctx_nat, ctx_T, last_T, wkT, wv, q_dram, v_hi, v_lo, o_hi, o_lo, identity, HEADS)
    head_attention(nc, x, w_out, b_out, gate, (aq, ak, av), o_hi, o_lo, qkv, mixed, x2, identity, block_mask)
    gated_mlp(nc, x2, wg, wu, wd, out, identity, 1.0 / 127.0)


def kernel(**inputs):
    import numpy as np
    import concourse.bacc as bacc
    from concourse.bass_utils import run_bass_kernel_spmd

    a = {k: np.asarray(v) for k, v in inputs.items()}
    B, SQ, dim = a["x"].shape
    inner = a["L0_xattn_w_q"].shape[1]
    ctx = a["ctx_1024"]
    w_kv = a["L0_xattn_w_kv"]
    heads = 16
    laid = {
        "x": a["x"].reshape(B * SQ, dim),
        "ctx_nat": ctx,
        "ctx_T": ctx.transpose(0, 2, 1),
        "last_T": ctx[:, -1, :].T,
        "gamma": a["L0_xattn_ln_gamma"].reshape(-1, P).T,
        "beta": a["L0_xattn_ln_beta"].reshape(-1, P).T,
        "wq": a["L0_xattn_w_q"],
        "wkT": w_kv[:, :inner].T,
        "wv": w_kv[:, inner:],
        "w_out": a["L0_xattn_w_out"],
        "b_out": a["L0_xattn_b_out"],
        "gate": a["L0_xattn_gate"],
        "aq": a["L0_attn_W_Q"].T,
        "ak": a["L0_attn_W_K"].T,
        "av": a["L0_attn_W_V"].T,
        "wg": a["L0_ffn_w_gate"].T,
        "wu": a["L0_ffn_w_up"].T,
        "wd": a["L0_ffn_w_down"].T,
        "identity": np.eye(P, dtype=np.float32),
        "block_mask": np.kron(np.eye(P // heads, dtype=np.float32), np.ones((heads, heads), np.float32)),
    }
    laid = {k: np.ascontiguousarray(v) for k, v in laid.items()}
    nc = bacc.Bacc("TRN2", target_bir_lowering=False, num_devices=1)
    aps = {k: nc.dram_tensor(k, v.shape, mybir.dt.from_np(v.dtype), kind="ExternalInput").ap() for k, v in laid.items()}
    out = nc.dram_tensor("out", [B * SQ, dim], F32, kind="ExternalOutput").ap()
    build(nc, out=out, **aps)
    r = run_bass_kernel_spmd(nc, [laid], core_ids=[0])
    return r.results[0]["out"].reshape(B, SQ, dim)
```
